# Optimizing a Trainium2 kernel written in Bass

```python
import numpy as np
import jax
import jax.numpy as jnp

def _softmax(x, axis=-1):
    return jax.nn.softmax(x, axis=axis)

def _gelu(x):
    return jax.nn.gelu(x, approximate=True)

def _silu(x):
    return jax.nn.silu(x)

def _sigmoid(x):
    return jax.nn.sigmoid(x)

def _layernorm(x, axis=-1, eps=1e-05):
    m = jnp.mean(x, axis=axis, keepdims=True)
    v = jnp.var(x, axis=axis, keepdims=True)
    return (x - m) / jnp.sqrt(v + eps)

def _scatter_add(tgt, idx, src, axis=0):
    return tgt.at[idx].add(src)

def _segment_sum(src, seg, n):
    return jax.ops.segment_sum(src, seg, n)
kernel_name = 'mk_xattn_ffn_d1_seqx_r4_d0751e'

def setup_inputs(seed: int=0):
    np.random.seed(seed)
    _w = jnp.asarray

    def _rec_inputs():
        import jax
        import jax.numpy as jnp
        _rk = jax.random.key(seed)
        x = -0.000125 + 0.9999 * jax.random.normal(jax.random.fold_in(_rk, 1), (16, 256, 256), jnp.float32)
        _lenS = 256 - jax.random.randint(jax.random.fold_in(_rk, 7), (16,), 0, max(1, 256 // 4) + 1, jnp.int32)
        _lenS2 = 256 - jax.random.randint(jax.random.fold_in(_rk, 8), (16,), 0, max(1, 256 // 4) + 1, jnp.int32)
        _ctx_1024P = jax.random.normal(jax.random.fold_in(_rk, 11), (16, 16, 256), jnp.float32)
        _ctx_1024c = jax.random.dirichlet(jax.random.fold_in(_rk, 511), 0.3 * jnp.ones((16,), jnp.float32), (16, 256))
        _ctx_1024t = jnp.einsum('bsk,bkd->bsd', _ctx_1024c, _ctx_1024P)
        _ctx_1024t = _ctx_1024t * jax.lax.rsqrt(jnp.mean(jnp.square(_ctx_1024t)) + 1e-12) * 0.953939
        ctx_1024 = -1.52775e-05 + 0.999936 * (_ctx_1024t + 0.3 * jax.random.normal(jax.random.fold_in(_rk, 611), (16, 256, 256), jnp.float32))
        return (x, ctx_1024)
    x, ctx_1024 = _rec_inputs()

    def _L0_xattn_setup():
        import jax, jax.numpy as jnp
        import numpy as np
        import math
        NHEADS = 16
        CAUSAL = True
        NEG_INF = -1e+18
        key = jax.random.key(seed)
        kq, kk, kv = jax.random.split(key, 3)
        B, S, D = (4, 2048, 256)
        q = jax.random.normal(kq, (B, S, D), dtype=jnp.float32)
        k = jax.random.normal(kk, (B, S, D), dtype=jnp.float32)
        v = jax.random.normal(kv, (B, S, D), dtype=jnp.float32)
        return {'q': q, 'k': k, 'v': v}
    _L0_xattn_all = _L0_xattn_setup()
    _L0_xattn_in = {k: v for k, v in _L0_xattn_all.items() if k in ()}
    del _L0_xattn_all

    def _L0_ffn_setup():
        import jax, jax.numpy as jnp
        import numpy as np
        B, S, D, H, E = (4, 512, 256, 1024, 8)
        key = jax.random.key(seed)
        ks = jax.random.split(key, 8)
        s_d = 1.0 / np.sqrt(D)
        s_h = 1.0 / np.sqrt(H)
        return {'x': jax.random.normal(ks[0], (B, S, D), dtype=jnp.float32), 'gate_w': jax.random.uniform(ks[1], (E, D), jnp.float32, -s_d, s_d), 'gate_b': jax.random.uniform(ks[2], (E,), jnp.float32, -s_d, s_d), 'w1': jax.random.uniform(ks[3], (E, H, D), jnp.float32, -s_d, s_d), 'b1': jax.random.uniform(ks[4], (E, H), jnp.float32, -s_d, s_d), 'w2': jax.random.uniform(ks[5], (E, D, H), jnp.float32, -s_h, s_h), 'b2': jax.random.uniform(ks[6], (E, D), jnp.float32, -s_h, s_h)}
    _L0_ffn_all = _L0_ffn_setup()
    _L0_ffn_in = {k: v for k, v in _L0_ffn_all.items() if k in ('gate_w', 'gate_b', 'w1', 'b1', 'w2', 'b2')}
    del _L0_ffn_all
    return {'x': x, 'ctx_1024': ctx_1024, 'L0_ffn_gate_w': _L0_ffn_in['gate_w'], 'L0_ffn_gate_b': _L0_ffn_in['gate_b'], 'L0_ffn_w1': _L0_ffn_in['w1'], 'L0_ffn_b1': _L0_ffn_in['b1'], 'L0_ffn_w2': _L0_ffn_in['w2'], 'L0_ffn_b2': _L0_ffn_in['b2']}

def reference(x, ctx_1024, L0_ffn_gate_w, L0_ffn_gate_b, L0_ffn_w1, L0_ffn_b1, L0_ffn_w2, L0_ffn_b2):
    import jax
    import jax.numpy as jnp

    def _L0_xattn_ref(q, k, v):
        import jax, jax.numpy as jnp
        import numpy as np
        import math
        NHEADS = 16
        CAUSAL = True
        NEG_INF = -1e+18
        B, S, D = q.shape
        hd = D // NHEADS
        qh = q.reshape(B, S, NHEADS, hd)
        kh = k.reshape(B, S, NHEADS, hd)
        vh = v.reshape(B, S, NHEADS, hd)
        scores = jnp.einsum('bsqd,bskd->bsqk', qh, kh) / math.sqrt(hd)
        if CAUSAL:
            mask = jnp.tril(jnp.ones((NHEADS, NHEADS), dtype=bool))
            scores = jnp.where(mask, scores, jnp.asarray(NEG_INF, scores.dtype))
        attn = jax.nn.softmax(scores, axis=-1)
        out = jnp.einsum('bsqk,bskd->bsqd', attn, vh)
        return out.reshape(B, S, D)

    def _L0_ffn_ref(x, gate_w, gate_b, w1, b1, w2, b2):
        import jax, jax.numpy as jnp
        import numpy as np
        B, S, D, H, E = (4, 512, 256, 1024, 8)
        b, s, d = x.shape
        xf = x.reshape(-1, d)
        logits = xf @ gate_w.T + gate_b
        top1 = jnp.argmax(logits, axis=-1)
        out = jnp.zeros_like(xf)
        n_experts = w1.shape[0]
        for e in range(n_experts):
            h = jax.nn.relu(xf @ w1[e].T + b1[e])
            y = h @ w2[e].T + b2[e]
            out = out + jnp.where((top1 == e)[:, None], y, jnp.zeros((), y.dtype))
        return out.reshape(b, s, d)
    x = x + _L0_xattn_ref(_layernorm(x, axis=-1), ctx_1024, ctx_1024)
    x = x + _L0_ffn_ref(_layernorm(x, axis=-1), L0_ffn_gate_w, L0_ffn_gate_b, L0_ffn_w1, L0_ffn_b1, L0_ffn_w2, L0_ffn_b2)
    return x

_drawn_inputs = setup_inputs


def setup_inputs(seed=0):
    import zlib

    import numpy as np

    out = dict(_drawn_inputs(seed))
    spreads = {}
    factors = {'L0_ffn_b1': 5.159, 'L0_ffn_b2': 4.053}
    for name, (base, spread) in spreads.items():
        noise = np.random.default_rng([zlib.crc32(name.encode()), seed]).standard_normal(out[name].shape)
        drawn = base * np.exp(spread * noise) if base else spread * noise
        out[name] = jnp.asarray(drawn.astype(out[name].dtype))
    for name, factor in factors.items():
        out[name] = (out[name] * factor).astype(out[name].dtype)
    return out
```

```python
from contextlib import ExitStack

import numpy as np

import concourse.bass as bass
from concourse import mybir

F32 = mybir.dt.float32
BF16 = mybir.dt.bfloat16
I32 = mybir.dt.int32
ALU = mybir.AluOpType
ACT = mybir.ActivationFunctionType
AX_X = mybir.AxisListType.X

P = 128
HEADS = 16
EPS = 1e-5
MASKED = -4e18
G = 2
SKIPPED_ROW = 1 << 20


class Mark:

    def __init__(self, sem, value):
        self.sem, self.value = sem, value


class Queue:

    def __init__(self, sem):
        self.sem, self.steps, self.count = sem, [], 0

    def put(self, waits, issue):
        self.count += 1
        self.steps.append((waits, issue, self.sem, 1))
        return Mark(self.sem, self.count)

    def dma(self, waits, issue, sem, value):
        self.steps.append((waits, issue, sem, 16))
        return Mark(sem, value)

    def run(self, engine):
        seen = {}
        for waits, issue, sem, inc in self.steps:
            for m in waits:
                if m is not None and seen.get(m.sem, 0) < m.value:
                    engine.wait_ge(m.sem, m.value)
                    seen[m.sem] = m.value
            last = issue(engine)
            if last is not None:
                last.then_inc(sem, inc)


def xattn_moe_kernel(nc, x, ctx_in, gate_w, gate_b, w1, b1, w2, b2, out):
    T, D = x.shape
    E = gate_b.shape[1]
    H = w1.shape[2] // 2
    HD = D // HEADS
    KD, KH = D // P, H // P
    NT = T // P
    NG = NT // G
    BANDS = HEADS // 2
    NTILES = NT + E - 1
    STRIDE = T + 2 * P
    ROW = D + 4
    HALF = 512

    def band_size(b):
        return 2 * G * (2 * b + 2) * HD

    sorted_rows = nc.dram_tensor("sorted_rows", [E * STRIDE, ROW], F32).ap()
    bias_rows = nc.dram_tensor("bias_rows", [E, 3, H + D], BF16).ap()

    stack = ExitStack()
    with stack:
        def sb(name, shape, dt=F32):
            return stack.enter_context(nc.sbuf_tensor(name, shape, dt))

        def ps(name):
            return stack.enter_context(nc.psum_tensor(name, [P, HALF], F32))

        def sem(name):
            return stack.enter_context(nc.semaphore(name))

        ident = sb("ident", [P, P])
        before = sb("before", [P, P], BF16)
        ones_bf = sb("ones_bf", [P, P], BF16)
        ones_row = sb("ones_row", [1, P])
        minus_half = sb("minus_half", [P, G])
        first_wins = sb("first_wins", [P, G, E])
        region = sb("region", [P, G, E])
        gate_sb = sb("gate_sb", [P, KD, E])
        gate_b_sb = sb("gate_b_sb", [1, E])
        w1_sb = sb("w1_sb", [P, E * KD * H])
        w2_sb = sb("w2_sb", [P, E * KH * D])
        XR = 4
        x_sb = sb("x_sb", [P, XR, G * D])
        c_sb = sb("c_sb", [P, 2, G * D])
        vt_sb = sb("vt_sb", [P, 2, G * D])
        q_sb = sb("q_sb", [P, G * D])
        a_sb = sb("a_sb", [P, 2, G * D])
        s_sb = sb("s_sb", [P, G * D])
        o_sb = sb("o_sb", [P, G * D])
        d_sb = sb("d_sb", [P, G * D])
        POOL_BANDS = {"qk": (7, 6), "pv": (7, 6)}
        DVE_BANDS = {k: tuple(b for b in reversed(range(BANDS)) if b not in v) for k, v in POOL_BANDS.items()}
        prod = sb("prod", [P, 2, max(band_size(b) for v in DVE_BANDS.values() for b in v)])
        pprod_at, n = {}, 0
        for kind, bands in POOL_BANDS.items():
            for b in bands:
                pprod_at[kind, b] = n
                n += band_size(b)
        pprod = sb("pprod", [P, n])
        junk = sb("junk", [P, 2, D], BF16)
        xstat = sb("xstat", [P, 2, 4, G])
        rowmax = sb("rowmax", [P, 2, HEADS * G])
        rowsum = sb("rowsum", [P, 2, HEADS * G])
        pay = sb("pay", [P, 2, G, ROW])
        stat1 = sb("stat1", [P, 2, 4, G])
        xn1 = sb("xn1", [P, G * D])
        xt1 = xn1
        route = sb("route", [P, 6, G * E])
        top = sb("top", [P, 2, G])
        onehot = sb("onehot", [P, NT, E], BF16)
        seen = sb("seen", [P, NT + 1, E], BF16)
        slot_f = sb("slot_f", [P, G])
        slot_i = sb("slot_i", [P, 2, G], I32)
        used = sb("used", [1, E])
        left = sb("left", [1, E])
        pick_hot = sb("pick_hot", [1, E])
        pick_v = sb("pick_v", [1, 4])
        plan = sb("plan", [1, NTILES], I32)
        count_i = sb("count_i", [1, E], I32)
        FR = 2
        rows = sb("rows", [P, FR, ROW])
        brow = sb("brow", [3, FR, H + D], BF16)
        xn2 = sb("xn2", [P, D])
        xt2 = sb("xt2", [P, D])
        h_sb = sb("h_sb", [P, H])
        ht_sb = sb("ht_sb", [P, H])
        y_sb = sb("y_sb", [P, 2, D])

        q_ps, a_ps, r_ps, m_ps, h0_ps, h1_ps, t0_ps, t1_ps = [ps(n) for n in
            ("q_ps", "a_ps", "r_ps", "m_ps", "h0_ps", "h1_ps", "t0_ps", "t1_ps")]
        h_ps, t_ps = (h0_ps, h1_ps), (t0_ps, t1_ps)
        xt2_ps, y_ps = m_ps[:, 0:D], m_ps[:, D:2 * D]

        pe, act, dve, pool, sp = [Queue(sem(n)) for n in ("s_pe", "s_act", "s_dve", "s_pool", "s_sp")]
        s_x = [sem(f"s_x{n}") for n in range(XR)]
        s_c = [sem(f"s_c{n}") for n in range(2)]
        s_w = sem("s_w")
        s_gate = sem("s_gate")
        s_bias_in = sem("s_bias_in")
        s_bias_out = sem("s_bias_out")
        s_scatter = [sem(f"s_scatter{n}") for n in range(2)]
        s_fill = sem("s_fill")
        s_rows = [sem(f"s_rows{n}") for n in range(FR)]
        s_brow = [sem(f"s_brow{n}") for n in range(FR)]
        s_out = [sem(f"s_out{n}") for n in range(2)]

        M = {}

        def done(step, n, *rest):
            return None if n < 0 else M[(step, n, *rest)]

        x_v = x.rearrange("(i p g) d -> i p (g d)", p=P, g=G)
        c_v = ctx_in.rearrange("(i p g) d -> i p (g d)", p=P, g=G)

        def load(i):
            r = i % XR
            M["x", i] = sp.dma([done("x1", i - XR)], lambda e: e.dma_start(x_sb[:, r, :], x_v[i]),
                               s_x[r], 16 * (i // XR + 1))

        def load_context(i):
            c = i % 2
            M["c", i] = sp.dma([done("qk", i - 2), done("qk_pool", i - 2), done("vt", i - 2)],
                               lambda e: e.dma_start(c_sb[:, c, :], c_v[i]), s_c[c], 16 * (i // 2 + 1))

        def load_weights():
            n = 0
            for e in range(E):
                for dst, src in ((w1_sb, w1), (w2_sb, w2)):
                    w = src.shape[2]
                    n += 16
                    M["weights"] = sp.dma([], lambda eng, dst=dst, src=src, e=e, w=w: eng.dma_start(
                        dst[:, e * w:(e + 1) * w], src[:, e, :]), s_w, n)

        def load_small():
            M["gate"] = sp.dma([], lambda e: e.dma_start(gate_sb[:], gate_w), s_gate, 32)
            sp.dma([], lambda e: e.dma_start(gate_b_sb[:], gate_b), s_gate, 32)
            bias = h_sb[0:E, :], ht_sb[0:E, 0:D]
            sp.dma([], lambda e: e.dma_start(bias[0], b1), s_bias_in, 32)
            M["bias"] = sp.dma([], lambda e: e.dma_start(bias[1], b2), s_bias_in, 32)

        def constants():
            pool.put([], lambda e: e.memset(ident[:], 1.0))
            k = pool.put([], lambda e: e.memset(ones_bf[:], 1.0))
            M["ident"] = pool.put([k], lambda e: e.affine_select(
                out=ident[:], in_=ident[:], compare_op=ALU.is_equal, fill=0.0, base=0,
                pattern=[[-1, P]], channel_multiplier=1))
            M["before"] = pool.put([k], lambda e: e.affine_select(
                out=before[:], in_=ones_bf[:], compare_op=ALU.is_gt, fill=0.0, base=0,
                pattern=[[1, P]], channel_multiplier=-1))
            dve.put([], lambda e: e.memset(minus_half[:], -0.5))
            dve.put([], lambda e: e.memset(ones_row[:], 1.0))
            dve.put([], lambda e: e.memset(seen[:, 0, :], 0.0))
            M["masked"] = dve.put([], lambda e: e.memset(s_sb[:], MASKED))
            for e_ in range(E):
                dve.put([], lambda e, e_=e_: e.memset(first_wins[:, :, e_], float(E - e_)))
                dve.put([], lambda e, e_=e_: e.memset(region[:, :, e_], float(e_ * STRIDE)))
                M["consts"] = dve.put([], lambda e, e_=e_: e.memset(used[:, e_:e_ + 1], float(E - 1 - e_) / E))

        def split_biases():
            parts = [bias_parts[:, n, :] for n in range(3)]
            W = H + D
            wide = bias_wide
            k = dve.put([M["bias"]], lambda e: e.tensor_copy(wide[:, 0:H], h_sb[0:E, :]))
            k = dve.put([k], lambda e: e.tensor_copy(wide[:, H:W], ht_sb[0:E, 0:D]))
            for n in range(3):
                k = dve.put([k], lambda e, n=n: e.tensor_copy(parts[n], wide[:, 0:W]))
                if n < 2:
                    k = dve.put([k], lambda e, n=n: e.tensor_tensor(wide[:, 0:W], wide[:, 0:W], parts[n], ALU.subtract))
            for n in range(3):
                M["bias_rows"] = sp.dma([k], lambda e, n=n: e.dma_start(bias_rows[:, n, :], parts[n]), s_bias_out, 48)

        bias_wide = pprod[0:E, 0:H + D]
        bias_parts = pprod[0:E, H + D:H + D + 3 * (H + D) // 2].bitcast(BF16).rearrange("p (n w) -> p n w", n=3)

        def ln_stats(src, st, i, name, ready):
            for g in range(G):
                k = M["junk", g] = act.put(ready + [done(name + "_shift", i - 2), M.get(("junk", g))], lambda e, g=g: e.activation(
                    junk[:, g], src(g), ACT.Identity, accum_out=st[:, 0, g:g + 1]))
            k = pool.put([k], lambda e: e.tensor_scalar(st[:, 0, :], st[:, 0, :], -1.0 / D, 0.0, ALU.mult, ALU.add))
            for g in range(G):
                k2 = M["junk", g] = act.put([k, M.get(("junk", g))], lambda e, g=g: e.activation(
                    junk[:, g], src(g), ACT.Square, bias=st[:, 0, g:g + 1], accum_out=st[:, 1, g:g + 1]))
            k = pool.put([k2], lambda e: e.tensor_scalar(st[:, 1, :], st[:, 1, :], 1.0 / D, EPS, ALU.mult, ALU.add))
            return k

        def xstats(i):
            st = xstat[:, i % 2]
            x_g = lambda g: x_sb[:, i % XR, g * D:(g + 1) * D]
            k = ln_stats(x_g, st, i, "q", [M["x", i], done("q_psum", i - 2), done("q", i - 2)])
            k = pool.put([k, M["consts"]], lambda e: e.tensor_tensor(st[:, 2, :], st[:, 1, :], minus_half[:], ALU.pow))
            M["q_shift", i] = pool.put([k], lambda e: e.tensor_tensor(st[:, 3, :], st[:, 0, :], st[:, 2, :], ALU.mult))

        def normalise_q(i, dst, waits):
            st = xstat[:, i % 2]
            for g in range(G):
                o = dst.rearrange("p (h g d) -> p g h d", h=HEADS, g=G)[:, g]
                s = x_sb[:, i % XR, g * D:(g + 1) * D].rearrange("p (h d) -> p h d", h=HEADS)
                k = act.put([M["q_shift", i]] + waits, lambda e, g=g, o=o, s=s: e.activation(
                    o, s, ACT.Identity, scale=st[:, 2, g:g + 1], bias=st[:, 3, g:g + 1]))
            return k

        def queries(i):
            M["q", i] = normalise_q(i, q_sb[:], [done("qk_pool", i - 1)])

        def queries_psum(i):
            M["q_psum", i] = normalise_q(i, q_ps[:], [done("qk", i - 1)])

        def values(i):
            v = c_sb[:, i % 2, :].rearrange("p (g k d) -> p g d k", g=G, k=HEADS)
            o = vt_sb[:, i % 2, :].rearrange("p (g d k) -> p g d k", g=G, k=HEADS)
            for g in range(G):
                M["vt", i] = act.put([M["c", i], done("pv", i - 2), done("pv_pool", i - 2)],
                                     lambda e, g=g: e.copy(o[:, g], v[:, g]))

        def qk_operands(b, q, c):
            K = 2 * b + 2
            q_ = q[:, 2 * b * G * HD:(2 * b + 2) * G * HD].rearrange("p (qg d) -> p qg d", d=HD)
            q_ = q_.unsqueeze(2).to_broadcast([P, 2 * G, K, HD])
            c_ = c.rearrange("p (g k d) -> p g (k d)", g=G, k=HEADS)[:, :, 0:K * HD]
            c_ = c_.unsqueeze(1).to_broadcast([P, 2, G, K * HD])
            return q_, c_, 2 * G * K * HD

        def pv_operands(b, a, v):
            K = 2 * b + 2
            a_ = a[:, 2 * b * G * HEADS:(2 * b + 2) * G * HEADS].rearrange("p (qg k) -> p qg k", k=HEADS)[:, :, 0:K]
            a_ = a_.unsqueeze(2).to_broadcast([P, 2 * G, HD, K])
            v_ = v.rearrange("p (gd k) -> p gd k", k=HEADS)[:, :, 0:K]
            v_ = v_.unsqueeze(1).to_broadcast([P, 2, G * HD, K])
            return a_, v_, 2 * G * K * HD

        def product(engine, waits, dst, ops, kind):
            a_, b_, n = ops
            o = dst[:, 0:n]
            K = n // (2 * G * HD)
            if kind == "qk":
                o = o.rearrange("p (qg k d) -> p qg k d", qg=2 * G, k=K)
            else:
                o = o.rearrange("p (qg d k) -> p qg d k", qg=2 * G, k=K)
            return engine.put(waits, lambda e: e.tensor_tensor(o, a_, b_, ALU.mult))

        prod_free = [None] * 2
        prod_next = [0]
        pprod_free = {}

        def pool_products(kind, i):
            if kind == "qk":
                ready, ops = [M["q", i], M["c", i]], lambda b: qk_operands(b, q_sb[:], c_sb[:, i % 2, :])
            else:
                ready, ops = [M["a", i], M["vt", i]], lambda b: pv_operands(b, a_sb[:, i % 2, :], vt_sb[:, i % 2, :])
            for b in POOL_BANDS[kind]:
                dst = pprod[:, pprod_at[kind, b]:]
                M[kind + "_pool_band", i, b] = product(
                    pool, ready + [pprod_free.get((kind, b), M["bias_rows"])], dst, ops(b), kind)
            M[kind + "_pool", i] = M[kind + "_pool_band", i, POOL_BANDS[kind][-1]]

        def reduce_band(kind, i, b, src, waits):
            K = 2 * b + 2
            n = 2 * G * K * HD
            if kind == "qk":
                o = s_sb[:, 2 * b * G * HEADS:(2 * b + 2) * G * HEADS] \
                    .rearrange("p (qg k) -> p qg k", k=HEADS)[:, :, 0:K]
                v = src[:, 0:n].rearrange("p (qg k d) -> p qg k d", k=K, d=HD)
            else:
                o = o_sb[:, 2 * b * G * HD:(2 * b + 2) * G * HD]
                v = src[:, 0:n].rearrange("p (qgd k) -> p qgd k", k=K)
            return dve.put(waits, lambda e: e.tensor_reduce(o, v, AX_X, ALU.add))

        def vector_bands(kind, i, between):
            if kind == "qk":
                ready = [M["q_psum", i], M["c", i]]
                ops = lambda b: qk_operands(b, q_ps[:], c_sb[:, i % 2, :])
                free = [done("minus_max", i - 1), M["masked"]]
            else:
                ready = [M["a_psum", i], M["vt", i]]
                ops = lambda b: pv_operands(b, a_ps[:], vt_sb[:, i % 2, :])
                free = [done("attended", i - 1)]
            behind = None
            steps = []
            for b in DVE_BANDS[kind]:
                r = prod_next[0] % 2
                prod_next[0] += 1
                k = product(dve, ready + [prod_free[r]], prod[:, r, :], ops(b), kind)
                if behind is not None:
                    pb, pr, pk = behind
                    prod_free[pr] = reduce_band(kind, i, pb, prod[:, pr, :], [pk] + free)
                behind = (b, r, k)
                between()
            last_product = k
            M[kind, i] = last_product
            pb, pr, pk = behind
            pools = POOL_BANDS[kind]
            for n, b in enumerate(pools):
                k = reduce_band(kind, i, b, pprod[:, pprod_at[kind, b]:], [M[kind + "_pool_band", i, b]] + free)
                pprod_free[kind, b] = k
                if n == 0:
                    prod_free[pr] = k = reduce_band(kind, i, pb, prod[:, pr, :], [pk] + free)
                between()
            return dve_last()

        def dve_last():
            return Mark(dve.sem, dve.count)

        def scores(i, between):
            k = vector_bands("qk", i, between)
            st = s_sb[:]
            k = dve.put([k], lambda e: e.memset(diagonal(st), MASKED))
            M["max", i] = dve.put([k, done("minus_max", i - 2)], lambda e: e.tensor_reduce(
                rowmax[:, i % 2, :], st.rearrange("p (qg k) -> p qg k", k=HEADS), AX_X, ALU.max))

        def diagonal(st):
            a = st
            ap = [list(a.ap[0])] + [[2 * G * HEADS + 2, BANDS], [HEADS, G]]
            return bass.AP(tensor=a.tensor, offset=a.offset + 1, ap=ap)

        def subtract_max(i):
            st = s_sb[:].rearrange("p (qg k) -> p qg k", k=HEADS)
            mx = rowmax[:, i % 2, :].unsqueeze(2).to_broadcast([P, HEADS * G, HEADS])
            M["minus_max", i] = pool.put([M["max", i], done("a", i - 1), done("a_psum", i - 1)],
                                         lambda e: e.tensor_tensor(d_sb[:].rearrange("p (qg k) -> p qg k", k=HEADS), st, mx, ALU.subtract))

        SCALE = 1.0 / float(np.sqrt(HD))

        def softmax_sbuf(i):
            M["a", i] = act.put([M["minus_max", i], done("pv_pool", i - 2), done("sum", i - 2)],
                                lambda e: e.activation(a_sb[:, i % 2, :], d_sb[:], ACT.Exp, scale=SCALE))

        def softmax_psum(i):
            M["a_psum", i] = act.put([M["minus_max", i], done("pv", i - 1)],
                                     lambda e: e.activation(a_ps[:], d_sb[:], ACT.Exp, scale=SCALE))

        def weighted(i, between):
            a = a_sb[:, i % 2, :].rearrange("p (qg k) -> p qg k", k=HEADS)
            M["sum", i] = dve.put([M["a", i], done("attended", i - 2)], lambda e: e.tensor_reduce(
                rowsum[:, i % 2, :], a, AX_X, ALU.add))
            M["pv_sums", i] = vector_bands("pv", i, between)
            M["inverse", i] = dve.put([M["sum", i]], lambda e: e.reciprocal(rowsum[:, i % 2, :], rowsum[:, i % 2, :]))

        def residual(i):
            r = i % 2
            o = o_sb[:].rearrange("p (qg d) -> p qg d", d=HD)
            inv = rowsum[:, r, :].unsqueeze(2).to_broadcast([P, HEADS * G, HD])
            M["attended", i] = pool.put([M["pv_sums", i], M["inverse", i]],
                                        lambda e: e.tensor_tensor(o, o, inv, ALU.mult))
            for g in range(G):
                xo = x_sb[:, i % XR, g * D:(g + 1) * D].rearrange("p (q d) -> p q d", q=HEADS)
                oo = o_sb[:].rearrange("p (q g d) -> p g q d", q=HEADS, g=G)[:, g]
                po = pay[:, r, g, 0:D].rearrange("p (q d) -> p q d", q=HEADS)
                k = pool.put([M["attended", i], done("scatter", i - 2)],
                             lambda e, xo=xo, oo=oo, po=po: e.tensor_tensor(po, xo, oo, ALU.add))
            M["x1", i] = k
            M["attended", i] = k
            M["ids", i] = pool.put([], lambda e: e.iota(
                pay[:, r, :, :].bitcast(I32)[:, :, D + 2], pattern=[[1, G]], base=i * P * G, channel_multiplier=G))
            M["pad", i] = pool.put([], lambda e: e.memset(pay[:, r, :, D + 3], 0.0))

        def ln1(i):
            r = i % 2
            st = stat1[:, r]
            k = ln_stats(lambda g: pay[:, r, g, 0:D], st, i, "ln1", [M["x1", i]])
            k = pool.put([k], lambda e: e.tensor_tensor(pay[:, r, :, D + 1], st[:, 1, :], minus_half[:], ALU.pow))
            M["ln1_shift", i] = pool.put([k], lambda e: e.tensor_tensor(
                pay[:, r, :, D], st[:, 0, :], pay[:, r, :, D + 1], ALU.mult))

        def gate_in(i):
            r = i % 2
            for g in range(G):
                k = act.put([M["ln1_shift", i], done("logits", i - 1)], lambda e, g=g: e.activation(
                    xn1[:, g * D:(g + 1) * D], pay[:, r, g, 0:D], ACT.Identity,
                    scale=pay[:, r, g, D + 1:D + 2], bias=pay[:, r, g, D:D + 1]))
            M["xn1", i] = k

        def gate_t(i):
            for n in range(G * KD):
                k = pe.put([M["xn1", i], M["ident"], done("picked", i - 1)],
                           lambda e, n=n: e.transpose(r_ps[:, n * P:(n + 1) * P], xn1[:, n * P:(n + 1) * P], ident[:]))
            M["gate_t", i] = k

        def gate_copy(i):
            M["xt1", i] = act.put([M["gate_t", i], done("logits", i - 1)], lambda e: e.copy(xt1[:], r_ps[:]))

        LG = r_ps[:, 0:G * E]
        RK = r_ps[:, G * E:2 * G * E]
        CN = r_ps[:, 2 * G * E:2 * G * E + E]

        def logits(i):
            for g in range(G):
                o = LG[:, g * E:(g + 1) * E]
                for k_ in range(KD):
                    n = g * KD + k_
                    pe.put([M["xt1", i], M["gate"]], lambda e, n=n, k_=k_, o=o: e.matmul(
                        o, xt1[:, n * P:(n + 1) * P], gate_sb[:, k_, :], start=(k_ == 0), stop=False))
                k = pe.put([], lambda e, o=o: e.matmul(o, ones_row[:], gate_b_sb[:], start=False, stop=True))
            M["logits", i] = k

        def choose(i):
            v = [route[:, n, :].rearrange("p (g e) -> p g e", g=G) for n in range(6)]
            lg = LG.rearrange("p (g e) -> p g e", g=G)
            bc = lambda n: top[:, n, :].unsqueeze(2).to_broadcast([P, G, E])
            oh = onehot[:, i * G:(i + 1) * G, :]
            k = dve.put([M["logits", i]], lambda e: e.tensor_reduce(top[:, 0, :], lg, AX_X, ALU.max))
            k = dve.put([k], lambda e: e.tensor_tensor(v[0], lg, bc(0), ALU.is_ge))
            k = dve.put([k], lambda e: e.tensor_tensor(v[1], v[0], first_wins[:], ALU.mult))
            k = dve.put([k], lambda e: e.tensor_reduce(top[:, 1, :], v[1], AX_X, ALU.max))
            k = dve.put([k], lambda e: e.tensor_tensor(oh, v[1], bc(1), ALU.is_equal))
            for n in range(i * G, (i + 1) * G):
                k = dve.put([k], lambda e, n=n: e.tensor_tensor(seen[:, n + 1, :], seen[:, n, :], onehot[:, n, :], ALU.add))
            M["chosen", i] = k

        def rank(i):
            for g in range(G):
                n = i * G + g
                o = RK[:, g * E:(g + 1) * E]
                pe.put([M["chosen", i], M["before"]], lambda e, n=n, o=o: e.matmul(
                    o, before[:], onehot[:, n, :], start=True, stop=False))
                pe.put([], lambda e, n=n, o=o: e.matmul(o, ones_bf[:], seen[:, n, :], start=False, stop=True))
            M["ranked", i] = pe.put([], lambda e: e.matmul(CN, ones_bf[:], seen[:, (i + 1) * G, :], start=True, stop=True))

        def slots(i):
            v = [route[:, n, :].rearrange("p (g e) -> p g e", g=G) for n in range(6)]
            rk = RK.rearrange("p (g e) -> p g e", g=G)
            k = dve.put([M["ranked", i]], lambda e: e.tensor_tensor(v[2], rk, region[:], ALU.add))
            k = dve.put([k], lambda e: e.tensor_tensor(v[3], v[2], onehot[:, i * G:(i + 1) * G, :], ALU.mult))
            k = dve.put([k], lambda e: e.tensor_reduce(slot_f[:], v[3], AX_X, ALU.add))
            M["slots", i] = M["picked", i] = dve.put(
                [k, done("scatter", i - 2)], lambda e: e.tensor_copy(slot_i[:, i % 2, :], slot_f[:]))

        def scatter(i):
            r = i % 2
            for g in range(G):
                M["scatter", i] = pool.dma(
                    [M["slots", i], M["ids", i], M["pad", i], M["ln1_shift", i], M["x1", i], M["xn1", i]],
                    lambda e, g=g: e.indirect_dma_start(
                        out=sorted_rows, out_offset=bass.IndirectOffsetOnAxis(ap=slot_i[:, r, g:g + 1], axis=0),
                        in_=pay[:, r, g, :], in_offset=None, bounds_check=E * STRIDE - 1, oob_is_err=False),
                    s_scatter[r], 16 * G * (i // 2 + 1))

        def pick(j, i):
            k = dve.put([M["ranked", i], M["consts"], done("pick", j - 1)], lambda e: e.tensor_tensor_reduce(
                left[:], CN[0:1, :], used[:], 1.0, -1e9, ALU.add, ALU.max, pick_v[:, 0:1]))
            k = dve.put([k], lambda e: e.tensor_scalar(pick_hot[:], left[:], pick_v[:, 0:1], None, ALU.is_equal))
            k = dve.put([k], lambda e: e.tensor_tensor_reduce(
                left[:], pick_hot[:], used[:], 1.0, 0.0, ALU.mult, ALU.add, pick_v[:, 1:2]))
            M["plan", j] = dve.put([k], lambda e: e.tensor_scalar(
                plan[:, j:j + 1], pick_v[:, 1:2], -float(E), float(E - 1), ALU.mult, ALU.add))
            M["pick", j] = M["picked", i] = dve.put([k], lambda e: e.scalar_tensor_tensor(
                out=used[:], in0=pick_hot[:], scalar=-float(P), in1=used[:], op0=ALU.mult, op1=ALU.add))

        def fill():
            filler = prod[:, 0, 0:2 * ROW].rearrange("p (r c) -> p r c", r=2)
            k = pool.put([prod_free[0]], lambda e: e.memset(filler, 0.0))
            M["filler"] = pool.put([k], lambda e: e.memset(filler.bitcast(I32)[:, :, D + 2], SKIPPED_ROW))
            M["counts"] = dve.put([M["ranked", NG - 1]], lambda e: e.tensor_copy(count_i[:], CN[0:1, :]))
            for e_ in range(E):
                def issue(eng, e_=e_):
                    n = eng.value_load(count_i[0:1, e_:e_ + 1], min_val=0, max_val=T)
                    row = nc.snap(n + e_ * STRIDE, min_val=0, max_val=E * STRIDE - 2 * P)
                    return eng.dma_start(
                        sorted_rows[bass.ds(row, 2 * P), :].rearrange("(p r) c -> p r c", r=2), filler)
                M["filled"] = sp.dma([M["counts"], M["filler"]], issue, s_fill, 16 * E)

        def fetch(j, i):
            r = j % FR
            waits = [M["plan", j], M["scatter", i], M["bias_rows"], done("y", j - FR), done("down", j - FR), done("stored", j - FR)]
            if i == NG - 1:
                waits += [M["filled"], M["scatter", i - 1]]

            def issue(eng):
                u = eng.value_load(plan[0:1, j:j + 1], min_val=0, max_val=E * (T + P))
                row = nc.snap((u & (E - 1)) * STRIDE + (u >> (E.bit_length() - 1)),
                              min_val=0, max_val=E * STRIDE - P)
                eng.dma_start(rows[:, r, :], sorted_rows[bass.ds(row, P), :]).then_inc(s_rows[r], 16)
                e_ = nc.snap(u & (E - 1), min_val=0, max_val=E - 1)
                return eng.dma_start(brow[:, r, :].unsqueeze(1), bias_rows[bass.ds(e_, 1), :, :]
                                     .rearrange("e n w -> n e w"))
            M["brow", j] = sp.dma(waits, issue, s_brow[r], 16 * (j // FR + 1))
            M["rows", j] = Mark(s_rows[r], 16 * (j // FR + 1))

        def expert_ln(j):
            r = j % FR
            M["xn2", j] = act.put([M["rows", j], done("expert_t", j - 1)], lambda e: e.activation(
                xn2[:], rows[:, r, 0:D], ACT.Identity, scale=rows[:, r, D + 1:D + 2], bias=rows[:, r, D:D + 1]))

        def expert_t(j):
            for k_ in range(KD):
                k = pe.put([M["xn2", j], done("xt2", j - 1), M["ident"]], lambda e, k_=k_: e.transpose(
                    xt2_ps[:, k_ * P:(k_ + 1) * P], xn2[:, k_ * P:(k_ + 1) * P], ident[:]))
            M["expert_t", j] = k

        def expert_copy(j):
            M["xt2", j] = act.put([M["expert_t", j], done("up", j - 1)],
                                  lambda e: e.copy(xt2[:], xt2_ps))

        pe_expert = {}

        def up(j):
            r = j % FR

            def first(eng):
                u = eng.value_load(plan[0:1, j:j + 1], min_val=0, max_val=E * (T + P))
                pe_expert[j] = nc.snap((u & (E - 1)) * (KD * H), min_val=0, max_val=(E - 1) * KD * H)
                return eng.matmul(h_ps[0][:], ones_bf[0:3, :], brow[:, r, 0:HALF], start=True, stop=False)
            for c in range(H // HALF):
                if c == 0:
                    pe.put([M["xt2", j], M["brow", j], M["weights"], M["plan", j], done("h", j - 1, 0)], first)
                else:
                    pe.put([done("h", j - 1, c)], lambda e, c=c: e.matmul(
                        h_ps[c][:], ones_bf[0:3, :], brow[:, r, c * HALF:(c + 1) * HALF], start=True, stop=False))
                for k_ in range(KD):
                    k = pe.put([], lambda e, c=c, k_=k_: e.matmul(
                        h_ps[c][:], xt2[:, k_ * P:(k_ + 1) * P],
                        w1_sb[:, bass.ds(pe_expert[j] + (k_ * H + c * HALF), HALF)],
                        start=False, stop=(k_ == KD - 1)))
                M["up_part", j, c] = k
            M["up", j] = k

        def relu(j):
            for c in range(H // HALF):
                M["h", j, c] = act.put([M["up_part", j, c], done("h_t", j - 1)], lambda e, c=c: e.activation(
                    h_sb[:, c * HALF:(c + 1) * HALF], h_ps[c][:], ACT.Relu))

        def turn(j):
            for c in range(H // HALF):
                for n in range(HALF // P):
                    s = c * HALF + n * P
                    k = pe.put([M["h", j, c], done("ht", j - 1, c)], lambda e, c=c, n=n, s=s: e.transpose(
                        t_ps[c][:, n * P:(n + 1) * P], h_sb[:, s:s + P], ident[:]))
                M["h_t_part", j, c] = k
            M["h_t", j] = k

        def turned(j):
            for c in range(H // HALF):
                M["ht", j, c] = act.put([M["h_t_part", j, c], done("down", j - 1)], lambda e, c=c: e.copy(
                    ht_sb[:, c * HALF:(c + 1) * HALF], t_ps[c][:]))

        def down(j):
            r = j % FR
            pe.put([done("y", j - 1), M["ht", j, 0]], lambda e: e.matmul(
                y_ps, ones_bf[0:3, :], brow[:, r, H:H + D], start=True, stop=False))
            for n in range(KH):
                k = pe.put([M["ht", j, n * P // HALF]], lambda e, n=n: e.matmul(
                    y_ps, ht_sb[:, n * P:(n + 1) * P], w2_sb[:, bass.ds(pe_expert[j] + n * D, D)],
                    start=False, stop=(n == KH - 1)))
            M["down", j] = k

        def result(j):
            M["y", j] = dve.put([M["down", j], done("stored", j - 2)], lambda e: e.tensor_tensor(
                y_sb[:, j % 2, :], y_ps, rows[:, j % FR, 0:D], ALU.add))

        def store(j):
            r = j % 2
            M["stored", j] = pool.dma([M["y", j]], lambda e: e.indirect_dma_start(
                out=out, out_offset=bass.IndirectOffsetOnAxis(
                    ap=rows[:, j % FR, :].bitcast(I32)[:, D + 2:D + 3], axis=0),
                in_=y_sb[:, r, :], in_offset=None, bounds_check=T - 1, oob_is_err=False),
                s_out[r], 16 * (j // 2 + 1))

        assert KD * H == KH * D

        def picks_after(i):
            n = (i + 1) * G * P
            if i == NG - 1:
                return NTILES
            return max(0, (n - E * (P - 1) - 1) // P + 1) if n > E * (P - 1) else 0

        group_of = {}
        for i in range(NG):
            for j in range(picks_after(i)):
                group_of.setdefault(j, i)

        constants()
        load_small()
        split_biases()
        load(0)
        load_context(0)
        load(1)
        load_context(1)
        load_weights()
        xstats(0)
        queries(0)
        queries_psum(0)
        values(0)
        xstats(1)
        pool_products("qk", 0)

        state = {"unit": 0, "picked": 0, "fetched": 0}

        def expert_unit():
            j = state["unit"]
            if j > NTILES or (j < NTILES and ("rows", j) not in M):
                return False
            if j == 0:
                expert_ln(0)
                expert_t(0)
                expert_copy(0)
            if j < NTILES:
                up(j)
            if j + 1 < NTILES and ("rows", j + 1) in M:
                expert_ln(j + 1)
                expert_t(j + 1)
            if j < NTILES:
                relu(j)
            if ("expert_t", j + 1) in M:
                expert_copy(j + 1)
            if j > 0:
                down(j - 1)
                result(j - 1)
                store(j - 1)
            if j < NTILES:
                turn(j)
                turned(j)
            state["unit"] += 1
            return True

        def late_expert_ln():
            j = state["unit"]
            if j > 0 and j < NTILES and ("rows", j) in M and ("xt2", j) not in M:
                expert_ln(j)
                expert_t(j)
                expert_copy(j)

        def fetch_ready(i):
            while state["fetched"] < state["picked"] and state["fetched"] < state["unit"] + FR - 1:
                j = state["fetched"]
                fetch(j, group_of[j])
                state["fetched"] += 1

        nothing = lambda: None
        for t in range(NG + 3):
            chain = []
            i = t - 2
            if 0 <= i < NG:
                residual(i)
                ln1(i)
                gate_in(i)
                gate_t(i)
                gate_copy(i)
                logits(i)
            if 1 <= t and t - 1 < NG:
                softmax_psum(t - 1)
                pool_products("pv", t - 1)
            if t < NG:
                if t + 2 < NG:
                    load(t + 2)
                scores(t, nothing)
                subtract_max(t)
                softmax_sbuf(t)
                if t + 2 < NG:
                    load_context(t + 2)
            if 0 <= i < NG:
                choose(i)
                rank(i)
                slots(i)
                scatter(i)
                for j in range(state["picked"], picks_after(i)):
                    pick(j, i)
                    state["picked"] = j + 1
                if i == NG - 1:
                    fill()
            fetch_ready(i)
            late_expert_ln()
            expert_unit()
            if t + 1 < NG:
                queries(t + 1)
                queries_psum(t + 1)
                pool_products("qk", t + 1)
            if t + 2 < NG:
                xstats(t + 2)
            if 1 <= t and t - 1 < NG:
                weighted(t - 1, nothing)
            if t + 1 < NG:
                values(t + 1)
            fetch_ready(i)
            late_expert_ln()
            expert_unit()
        while state["unit"] <= NTILES:
            fetch_ready(NG - 1)
            late_expert_ln()
            expert_unit()

        block = stack.enter_context(nc.Block())

        @block.sync
        def _(eng):
            sp.run(eng)
            for r in range(2):
                eng.wait_ge(s_out[r], 16 * ((NTILES - r + 1) // 2))

        @block.scalar
        def _(eng):
            act.run(eng)

        @block.vector
        def _(eng):
            dve.run(eng)

        @block.gpsimd
        def _(eng):
            pool.run(eng)

        @block.tensor
        def _(eng):
            pe.run(eng)


def kernel(x, ctx_1024, L0_ffn_gate_w, L0_ffn_gate_b, L0_ffn_w1, L0_ffn_b1, L0_ffn_w2, L0_ffn_b2):
    import concourse.bacc as bacc
    from concourse.bass_utils import run_bass_kernel_spmd

    B, S, D = x.shape
    E, H, _ = L0_ffn_w1.shape
    lay = np.ascontiguousarray
    arrays = {
        "x": lay(x).reshape(B * S, D),
        "ctx": lay(ctx_1024).reshape(B * S, D),
        "gate_w": lay(np.transpose(np.reshape(L0_ffn_gate_w, (E, D // P, P)), (2, 1, 0))),
        "gate_b": lay(np.reshape(L0_ffn_gate_b, (1, E))),
        "w1": lay(np.transpose(np.reshape(L0_ffn_w1, (E, H, D // P, P)), (3, 0, 2, 1))).reshape(P, E, (D // P) * H),
        "b1": lay(L0_ffn_b1),
        "w2": lay(np.transpose(np.reshape(L0_ffn_w2, (E, D, H // P, P)), (3, 0, 2, 1))).reshape(P, E, (H // P) * D),
        "b2": lay(L0_ffn_b2),
    }
    nc = bacc.Bacc("TRN2", target_bir_lowering=False, num_devices=1)
    args = [nc.dram_tensor(n, a.shape, mybir.dt.from_np(a.dtype), kind="ExternalInput").ap() for n, a in arrays.items()]
    res = nc.dram_tensor("result", (B * S, D), F32, kind="ExternalOutput").ap()
    xattn_moe_kernel(nc, *args, res)
    got = run_bass_kernel_spmd(nc, [arrays], core_ids=[0])
    return got.results[0]["result"].reshape(B, S, D)
```

```python
from contextlib import ExitStack

import numpy as np

import concourse.bass as bass
from concourse import mybir

F32 = mybir.dt.float32
F16 = mybir.dt.float16
BF16 = mybir.dt.bfloat16
I32 = mybir.dt.int32
ALU = mybir.AluOpType
ACT = mybir.ActivationFunctionType
AX_X = mybir.AxisListType.X

P = 128
HEADS = 16
EPS = 1e-5
MASKED = -4e18
W_SCALE = 64.0
G = 2
SKIPPED_ROW = 1 << 20


class Mark:

    def __init__(self, sem, value, at):
        self.sem, self.value, self.at = sem, value, at


class Queue:

    def __init__(self, sem):
        self.sem, self.steps, self.count, self.free = sem, [], 0, 0.0

    def run(self, engine):
        waited = {}
        for marks, issue, sem, inc in self.steps:
            for m in marks:
                if waited.get(m.sem, 0) < m.value:
                    engine.wait_ge(m.sem, m.value)
                    waited[m.sem] = m.value
            issue(engine).then_inc(sem, inc)


class Op:

    def __init__(self, queue, waits, issue, us, name=None, dma=None, kbytes=0):
        self.queue, self.waits, self.issue, self.us, self.name = queue, waits, issue, us, name
        self.dma, self.kbytes = dma, kbytes


class Order:

    WAKE = 0.13

    def __init__(self):
        self.marks, self.dma_free = {}, 0.0

    def start(self, op):
        at = op.queue.free
        for w in op.waits:
            if w is None:
                continue
            if not isinstance(w, Mark):
                if w[1] < 0:
                    continue
                if w not in self.marks:
                    return None
                w = self.marks[w]
            at = max(at, w.at + self.WAKE)
        return at

    def commit(self, op, at):
        marks = [w if isinstance(w, Mark) else self.marks[w] for w in op.waits
                 if w is not None and (isinstance(w, Mark) or w[1] >= 0)]
        q = op.queue
        q.free = at + op.us
        if op.dma:
            sem, value = op.dma
            q.steps.append((marks, op.issue, sem, 16))
            self.dma_free = max(self.dma_free, q.free + 0.8) + op.kbytes / 350.0
            m = Mark(sem, value, self.dma_free + 1.7)
        else:
            q.count += 1
            q.steps.append((marks, op.issue, q.sem, 1))
            m = Mark(q.sem, q.count, q.free)
        if op.name:
            self.marks[op.name] = m
        return m

    def merge(self, lanes):
        backs, lanes = zip(*lanes)
        wanted = [next(lane, None) for lane in lanes]
        while any(wanted):
            ready = [(self.start(op), n) for n, op in enumerate(wanted) if op is not None]
            ready = [(at + backs[n], n, at) for at, n in ready if at is not None]
            if not ready:
                raise RuntimeError(f"every lane waits: {[(n, o.name, o.waits) for n, o in enumerate(wanted) if o]}")
            _, n, at = min(ready)
            m = self.commit(wanted[n], at)
            try:
                wanted[n] = lanes[n].send(m)
            except StopIteration:
                wanted[n] = None


def xattn_moe_kernel(nc, x, ctx_in, gate_w, gate_b, w1, b1, w2, b2, out):
    T, D = x.shape
    E = gate_b.shape[1]
    H = w1.shape[2] * P // D
    HD = D // HEADS
    KD, KH = D // P, H // P
    NT = T // P
    NG = NT // G
    BANDS = HEADS // 2
    NTILES = NT + E - 1
    STRIDE = T + 2 * P
    ROW = D + 4
    HALF = 512
    SCALE = 1.0 / float(np.sqrt(HD))
    WC = H
    CHUNKS = 2 * E * KD * H // WC
    assert KD * H == KH * D

    dve_us = lambda n: 0.065 + n / 960
    act_us = lambda n: 0.21 + n / 1200
    pool_us = lambda n: 0.1 + n * 0.0021
    pe_us = lambda n: max(n, 64) / 2400 + 0.003
    pe32_us = lambda n: max(0.213, 4 * n / 2400)

    def band_size(b):
        return 2 * G * (2 * b + 2) * HD

    sorted_rows = nc.dram_tensor("sorted_rows", [E * STRIDE, ROW], F32).ap()
    BLOCKS = H // HALF + 1
    bias_rows = nc.dram_tensor("bias_rows", [E, BLOCKS * 3, HALF], BF16).ap()

    stack = ExitStack()
    with stack:
        def sb(name, shape, dt=F32):
            return stack.enter_context(nc.sbuf_tensor(name, shape, dt))

        def ps(name):
            return stack.enter_context(nc.psum_tensor(name, [P, HALF], F32))

        def sem(name):
            return stack.enter_context(nc.semaphore(name))

        ident = sb("ident", [P, P])
        minus_ident = sb("minus_ident", [P, P], F16)
        before = sb("before", [P, P], BF16)
        ones_bf = sb("ones_bf", [P, P], BF16)
        ones_row = sb("ones_row", [1, P])
        minus_half = sb("minus_half", [P, G])
        first_wins = sb("first_wins", [P, G, E])
        region = sb("region", [P, G, E])
        gate_sb = sb("gate_sb", [P, KD, E])
        gate_b_sb = sb("gate_b_sb", [1, E])
        w1_hi, w1_lo, w2_hi, w2_lo = [sb(n, [P, E * KD * H], F16) for n in ("w1_hi", "w1_lo", "w2_hi", "w2_lo")]
        XR = 4
        x_sb = sb("x_sb", [P, XR, G * D])
        c_sb = sb("c_sb", [P, 2, G * D])
        vt_sb = sb("vt_sb", [P, 2, G * D])
        q_sb = sb("q_sb", [P, G * D])
        a_sb = sb("a_sb", [P, 2, G * D])
        s_sb = sb("s_sb", [P, G * D])
        d_sb = sb("d_sb", [P, G * D])
        o_sb = sb("o_sb", [P, G * D])
        DVE_BANDS = (5, 0, 4, 1, 3, 2)
        PLACE = {5: (0, 3), 0: (768, 2), 4: (896, 2), 1: (0, 5), 3: (256, 5), 2: (768, 4)}
        TOP = 4
        TQ = HEADS - TOP
        TC = TOP * G * HEADS
        prod = sb("prod", [P, max(at + band_size(b) for b, (at, _) in PLACE.items())])
        pprod = sb("pprod", [P, 2, TC * HD])
        passed = sb("passed", [P, G, D], BF16)
        xstat = sb("xstat", [P, 2, 4, G])
        rowmax = sb("rowmax", [P, 2, HEADS * G])
        rowsum = sb("rowsum", [P, 2, HEADS * G])
        pay = sb("pay", [P, 2, G, ROW])
        stat1 = sb("stat1", [P, 2, 4, G])
        xn1 = sb("xn1", [P, G * D])
        route = sb("route", [P, 6, G * E])
        top = sb("top", [P, 2, G])
        onehot = sb("onehot", [P, NT, E], BF16)
        seen = sb("seen", [P, NT + 1, E], BF16)
        slot_f = sb("slot_f", [P, G])
        slot_i = sb("slot_i", [P, 2, G], I32)
        used = sb("used", [1, E])
        left = sb("left", [1, E])
        pick_hot = sb("pick_hot", [1, E])
        pick_v = sb("pick_v", [1, 4])
        plan = sb("plan", [1, NTILES], I32)
        count_i = sb("count_i", [1, E], I32)
        FR = 4
        rows = sb("rows", [P, FR, ROW])
        brow = sb("brow", [BLOCKS * 3, 2, HALF], BF16)
        block_sum = sb("block_sum", [BLOCKS * 3, BLOCKS, P], BF16)
        xn2 = sb("xn2", [P, D])
        xt_hi = sb("xt_hi", [P, D], F16)
        xt_lo = sb("xt_lo", [P, D], F16)
        h_parts = sb("h_parts", [P, 2 * 2 * H], F16)
        h_hi = [h_parts[:, n * 2 * H:n * 2 * H + H] for n in range(2)]
        h_lo = [h_parts[:, n * 2 * H + H:(n + 1) * 2 * H] for n in range(2)]
        w_in = [h_parts[:, n * 2 * WC:(n + 1) * 2 * WC].bitcast(F32) for n in range(2)]

        q_ps, a_ps, r_ps, m_ps, h0_ps, h1_ps, y_bank, top_ps = [ps(n) for n in
            ("q_ps", "a_ps", "r_ps", "m_ps", "h0_ps", "h1_ps", "y_ps", "top_ps")]
        h_ps = (h0_ps, h1_ps)
        xt2_ps, y_ps = m_ps[:, 0:D], y_bank[:, 0:D]
        LG = r_ps[:, 0:G * E]
        RK = r_ps[:, G * E:2 * G * E]
        CN = r_ps[:, 2 * G * E:2 * G * E + E]

        pe, act, dve, pool, sp = [Queue(sem(n)) for n in ("s_pe", "s_act", "s_dve", "s_pool", "s_sp")]
        s_x = [sem(f"s_x{n}") for n in range(XR)]
        s_c = [sem(f"s_c{n}") for n in range(2)]
        s_w = [sem(f"s_w{n}") for n in range(2)]
        s_gate, s_bias_in, s_bias_out, s_fill = [sem(n) for n in ("s_gate", "s_bias_in", "s_bias_out", "s_fill")]
        s_scatter = [sem(f"s_scatter{n}") for n in range(2)]
        s_rows = [sem(f"s_rows{n}") for n in range(FR)]
        s_brow = [sem(f"s_brow{n}") for n in range(2)]
        s_out = [sem(f"s_out{n}") for n in range(FR)]

        x_v = x.rearrange("(i p g) d -> i p (g d)", p=P, g=G)
        c_v = ctx_in.rearrange("(i p g) d -> i p (g d)", p=P, g=G)
        KB_GROUP = P * G * D * 4 / 1024

        def load_x():
            for i in range(NG):
                r = i % XR
                yield Op(sp, [("x1", i - XR)], lambda e, i=i, r=r: e.dma_start(x_sb[:, r, :], x_v[i]),
                         0.5, ("x", i), (s_x[r], 16 * (i // XR + 1)), KB_GROUP)

        def load_context():
            for i in range(NG):
                c = i % 2
                yield Op(sp, [("qk", i - 2), ("qk_pool", i - 2), ("vt", i - 2)],
                         lambda e, i=i, c=c: e.dma_start(c_sb[:, c, :], c_v[i]),
                         0.5, ("c", i), (s_c[c], 16 * (i // 2 + 1)), KB_GROUP)

        def weights():
            def load(n):
                src = (w1, w2)[n % 2].rearrange("p e w -> p (e w)")[:, n // 2 * WC:(n // 2 + 1) * WC]
                return Op(sp, [("weight_lo", n - 2, WC // HALF - 1)], lambda e: e.dma_start(w_in[n % 2], src),
                          0.5, ("weight_in", n), (s_w[n % 2], 16 * (n // 2 + 1)), P * WC * 4 / 1024)
            yield load(0)
            yield load(1)
            for n in range(CHUNKS):
                at = n // 2 * WC
                hi, lo = ((w1_hi, w1_lo), (w2_hi, w2_lo))[n % 2]
                high = yield Op(act, [("weight_in", n)], lambda e, n=n, hi=hi, at=at: e.activation(
                    hi[:, at:at + WC], w_in[n % 2], ACT.Copy, scale=W_SCALE), act_us(WC))
                if n % 2:
                    yield Op(dve, [high], lambda e, n=n, hi=hi, lo=lo, at=at: e.scalar_tensor_tensor(
                        out=lo[:, at:at + WC], in0=w_in[n % 2], scalar=W_SCALE, in1=hi[:, at:at + WC],
                        op0=ALU.mult, op1=ALU.subtract), dve_us(WC), ("weight_lo", n, WC // HALF - 1))
                    if n + 2 < CHUNKS:
                        yield load(n + 2)
                    continue
                for c in range(WC // HALF):
                    cols = slice(at + c * HALF, at + (c + 1) * HALF)
                    yield Op(pe, [("weight_in", n), ("weight_lo", n - 2, c), ("ident", 0)],
                             lambda e, n=n, c=c: e.matmul(
                                 h_ps[c][:], ident[:], w_in[n % 2][:, c * HALF:(c + 1) * HALF],
                                 start=True, stop=False), pe32_us(HALF))
                    k = yield Op(pe, [high, ("minus_ident", 0)], lambda e, c=c, hi=hi, cols=cols: e.matmul(
                        h_ps[c][:], minus_ident[:], hi[:, cols], start=False, stop=True), pe_us(HALF))
                    yield Op(act, [k], lambda e, c=c, lo=lo, cols=cols: e.activation(
                        lo[:, cols], h_ps[c][:], ACT.Copy, scale=W_SCALE),
                             act_us(HALF), ("weight_lo", n, c))
                if n + 2 < CHUNKS:
                    yield load(n + 2)
            M["weights", 0] = M["weight_lo", CHUNKS - 1, WC // HALF - 1]
            M["weights", 1] = M["weight_lo", CHUNKS - 2, WC // HALF - 1]

        def small_constants():
            k = yield Op(pool, [], lambda e: e.memset(ident[:], 1.0), 0.2)
            yield Op(pool, [k], lambda e: e.affine_select(
                out=ident[:], in_=ident[:], compare_op=ALU.is_equal, fill=0.0, base=0,
                pattern=[[-1, P]], channel_multiplier=1), 0.25, ("ident", 0))
            yield Op(pool, [("ident", 0)], lambda e: e.tensor_scalar(
                minus_ident[:], ident[:], -1.0 / W_SCALE, 0.0, ALU.mult, ALU.add), 0.25, ("minus_ident", 0))
            k = yield Op(pool, [], lambda e: e.memset(ones_bf[:], 1.0), 0.2)
            yield Op(pool, [k], lambda e: e.affine_select(
                out=before[:], in_=ones_bf[:], compare_op=ALU.is_gt, fill=0.0, base=0,
                pattern=[[1, P]], channel_multiplier=-1), 0.25, ("before", 0))
            yield Op(pool, [], lambda e: e.memset(minus_half[:], -0.5), 0.1, ("minus_half", 0))
            k = yield Op(pool, [], lambda e: e.memset(block_sum[:], 1.0), 0.3)
            k = yield Op(pool, [k], lambda e: e.affine_select(
                out=block_sum[:], in_=block_sum[:], compare_op=ALU.is_ge, fill=0.0, base=0,
                pattern=[[-3, BLOCKS], [0, P]], channel_multiplier=1), 0.5)
            yield Op(pool, [k], lambda e: e.affine_select(
                out=block_sum[:], in_=block_sum[:], compare_op=ALU.is_ge, fill=0.0, base=2,
                pattern=[[3, BLOCKS], [0, P]], channel_multiplier=-1), 0.5, ("block_sum", 0))
            yield Op(dve, [], lambda e: e.memset(s_sb[:], MASKED), 0.6, ("masked", 0))
            yield Op(dve, [], lambda e: e.memset(seen[:, 0, :], 0.0), 0.1)
            yield Op(dve, [], lambda e: e.memset(ones_row[:], 1.0), 0.1)
            for n in range(E):
                yield Op(dve, [], lambda e, n=n: e.memset(first_wins[:, :, n], float(E - n)), 0.1)
                yield Op(dve, [], lambda e, n=n: e.memset(region[:, :, n], float(n * STRIDE)), 0.1)
                yield Op(dve, [], lambda e, n=n: e.memset(used[:, n:n + 1], float(E - 1 - n) / E), 0.1,
                         ("tables", 0) if n == E - 1 else None)

        BW = BLOCKS * HALF
        setup = pprod[0:E].rearrange("p a b -> p (a b)")
        bias_wide = setup[:, 0:BW]
        bias_parts = setup[:, BW:BW + 3 * BW // 2].bitcast(BF16).rearrange("p (n w) -> p n w", n=3)

        def small_inputs():
            z = yield Op(dve, [], lambda e: e.memset(bias_wide[:, H + D:], 0.0), 0.1)
            yield Op(sp, [], lambda e: e.dma_start(bias_wide[:, 0:H], b1), 0.5, None, (s_bias_in, 32), 32)
            k = yield Op(sp, [], lambda e: e.dma_start(bias_wide[:, H:H + D], b2), 0.5, None, (s_bias_in, 32), 8)
            yield Op(sp, [], lambda e: e.dma_start(gate_sb[:], gate_w), 0.5, None, (s_gate, 32), 8)
            yield Op(sp, [], lambda e: e.dma_start(gate_b_sb[:], gate_b), 0.5, ("gate", 0), (s_gate, 32), 1)
            us = dve_us(BW)
            k = yield Op(dve, [k], lambda e: e.tensor_scalar(
                bias_wide[:, 0:H], bias_wide[:, 0:H], W_SCALE, None, ALU.mult), us)
            k = yield Op(dve, [k], lambda e: e.tensor_scalar(
                bias_wide[:, H:H + D], bias_wide[:, H:H + D], W_SCALE * W_SCALE, None, ALU.mult), us)
            for n in range(3):
                k = yield Op(dve, [k], lambda e, n=n: e.tensor_copy(bias_parts[:, n, :], bias_wide), us)
                if n < 2:
                    k = yield Op(dve, [k], lambda e, n=n: e.tensor_tensor(
                        bias_wide, bias_wide, bias_parts[:, n, :], ALU.subtract), us)
            for n in range(3):
                yield Op(sp, [k], lambda e, n=n: e.dma_start(
                    bias_rows.rearrange("e (c n) w -> e c n w", n=3)[:, :, n, :],
                    bias_parts[:, n, :].rearrange("e (c w) -> e c w", c=BLOCKS)),
                         0.5, ("bias_rows", 0), (s_bias_out, 48), 8)

        def ln_stats(src, st, passed, waits):
            for g in range(G):
                k = yield Op(act, waits, lambda e, g=g: e.activation(
                    passed(g), src(g), ACT.Identity, accum_out=st[:, 0, g:g + 1]), act_us(D) + 0.09)
            k = yield Op(pool, [k], lambda e: e.tensor_scalar(
                st[:, 0, :], st[:, 0, :], -1.0 / D, 0.0, ALU.mult, ALU.add), 0.16)
            for g in range(G):
                k2 = yield Op(act, [k], lambda e, g=g: e.activation(
                    passed(g), src(g), ACT.Square, bias=st[:, 0, g:g + 1], accum_out=st[:, 1, g:g + 1]),
                    act_us(D) + 0.09)
            k = yield Op(pool, [k2], lambda e: e.tensor_scalar(
                st[:, 1, :], st[:, 1, :], 1.0 / D, EPS, ALU.mult, ALU.add), 0.16)
            return k

        def x_stats():
            for i in range(NG):
                st = xstat[:, i % 2]
                x_g = lambda g, i=i: x_sb[:, i % XR, g * D:(g + 1) * D]
                k = yield from ln_stats(x_g, st, lambda g: passed[:, g],
                                        [("x", i), ("q_psum", i - 2), ("q", i - 2), ("q_shift", i - 1)])
                k = yield Op(pool, [k, ("minus_half", 0)], lambda e, st=st: e.tensor_tensor(
                    st[:, 2, :], st[:, 1, :], minus_half[:], ALU.pow), 0.63)
                yield Op(pool, [k], lambda e, st=st: e.tensor_tensor(
                    st[:, 3, :], st[:, 0, :], st[:, 2, :], ALU.mult), 0.15, ("q_shift", i))

        def queries(dst, name, frees):
            for i in range(NG):
                st = xstat[:, i % 2]
                for g in range(G):
                    o = dst.rearrange("p (h g d) -> p g h d", h=HEADS, g=G)[:, g]
                    s = x_sb[:, i % XR, g * D:(g + 1) * D].rearrange("p (h d) -> p h d", h=HEADS)
                    yield Op(act, [("q_shift", i)] + frees(i), lambda e, g=g, o=o, s=s, st=st: e.activation(
                        o, s, ACT.Identity, scale=st[:, 2, g:g + 1], bias=st[:, 3, g:g + 1]),
                        act_us(D) + 0.1, (name, i) if g == G - 1 else None)

        def turned_values():
            for i in range(NG):
                v = c_sb[:, i % 2, :].rearrange("p (g k d) -> p g d k", g=G, k=HEADS)
                o = vt_sb[:, i % 2, :].rearrange("p (g d k) -> p g d k", g=G, k=HEADS)
                for g in range(G):
                    yield Op(act, [("c", i), ("pv", i - 2), ("pv_pool", i - 2)],
                             lambda e, g=g, o=o, v=v: e.copy(o[:, g], v[:, g]), act_us(D),
                             ("vt", i) if g == G - 1 else None)

        def qk_operands(b, q, c):
            K = 2 * b + 2
            q_ = q[:, 2 * b * G * HD:(2 * b + 2) * G * HD].rearrange("p (qg d) -> p qg d", d=HD)
            c_ = c.rearrange("p (g k d) -> p g (k d)", g=G, k=HEADS)[:, :, 0:K * HD]
            return (q_.unsqueeze(2).to_broadcast([P, 2 * G, K, HD]),
                    c_.unsqueeze(1).to_broadcast([P, 2, G, K * HD]))

        def pv_operands(b, a, v):
            K = 2 * b + 2
            a_ = a[:, 2 * b * G * HEADS:(2 * b + 2) * G * HEADS].rearrange("p (qg k) -> p qg k", k=HEADS)[:, :, 0:K]
            v_ = v.rearrange("p (gd k) -> p gd k", k=HEADS)[:, :, 0:K]
            return (a_.unsqueeze(2).to_broadcast([P, 2 * G, HD, K]),
                    v_.unsqueeze(1).to_broadcast([P, 2, G * HD, K]))

        def product(kind, i, b, dst, waits, name):
            n, K = band_size(b), 2 * b + 2
            if kind == "qk":
                in0, in1 = qk_operands(b, q_ps[:], c_sb[:, i % 2, :])
                o = dst[:, 0:n].rearrange("p (qg k d) -> p qg k d", qg=2 * G, k=K)
            else:
                in0, in1 = pv_operands(b, a_ps[:], vt_sb[:, i % 2, :])
                o = dst[:, 0:n].rearrange("p (qg d k) -> p qg d k", qg=2 * G, k=K)
            return Op(dve, waits, lambda e: e.tensor_tensor(o, in0, in1, ALU.mult), dve_us(n), name)

        def band_sum(kind, i, b, src, waits, name):
            n, K = band_size(b), 2 * b + 2
            if kind == "qk":
                o = s_sb[:, 2 * b * G * HEADS:(2 * b + 2) * G * HEADS] \
                    .rearrange("p (qg k) -> p qg k", k=HEADS)[:, :, 0:K]
                v = src[:, 0:n].rearrange("p (qg k d) -> p qg k d", k=K, d=HD)
            else:
                o = o_sb[:, 2 * b * G * HD:(2 * b + 2) * G * HD]
                v = src[:, 0:n].rearrange("p (qgd k) -> p qgd k", k=K)
            return Op(dve, waits, lambda e: e.tensor_reduce(o, v, AX_X, ALU.add), dve_us(n), name)

        def top_products():
            def one(kind, i):
                if kind == "qk":
                    ready, dst = [("q", i), ("c", i), ("bias_rows", 0)], pprod[:, 0, :]
                    fixed = q_sb[:, TQ * G * HD:].rearrange("p (q g d) -> p q g d", q=TOP, g=G)
                    moving = c_sb[:, i % 2, :].rearrange("p (g kd) -> p g kd", g=G)
                else:
                    ready, dst = [("a", i), ("vt", i), ("bias_rows", 0)], pprod[:, 1, :]
                    fixed = a_sb[:, i % 2, TQ * G * HEADS:].rearrange("p (q g k) -> p q g k", q=TOP, g=G)
                    moving = vt_sb[:, i % 2, :].rearrange("p (g dk) -> p g dk", g=G)
                o = dst.rearrange("p (qg m n) -> p qg m n", qg=TOP * G, m=HEADS)
                fixed = fixed.rearrange("p q g n -> p (q g) n").unsqueeze(2).to_broadcast([P, TOP * G, HEADS, HD])
                moving = moving.unsqueeze(1).to_broadcast([P, TOP, G, HEADS * HD])
                return Op(pool, ready + [(kind + "_top_added", i - 1)],
                          lambda e: e.tensor_tensor(o, fixed, moving, ALU.mult), pool_us(TC * HD), (kind + "_pool", i))
            yield one("qk", 0)
            for i in range(NG):
                if i + 1 < NG:
                    yield one("qk", i + 1)
                yield one("pv", i)

        def top_sums():
            def one(kind, i, bank_read):
                src = pprod[:, ("qk", "pv").index(kind), :].rearrange("p (c n) -> p c n", n=HD)
                acc = top_ps[:, ("qk", "pv").index(kind) * TC:][:, 0:TC]
                for n in range(HD):
                    yield Op(pe, [(kind + "_pool", i), bank_read, ("ident", 0)],
                             lambda e, n=n: e.matmul(acc, ident[:], src[:, :, n], start=n == 0, stop=n == HD - 1),
                             pe32_us(TC), (kind + "_top_added", i) if n == HD - 1 else None)
                free, dst = [(("minus_max", i - 1), s_sb), (("attended", i - 1), o_sb)][kind == "pv"]
                return (yield Op(act, [(kind + "_top_added", i), free, ("masked", 0)],
                                 lambda e: e.copy(dst[:, TQ * G * HEADS:], acc), act_us(TC), (kind + "_top", i)))
            k = yield from one("qk", 0, None)
            for i in range(NG):
                if i + 1 < NG:
                    k = yield from one("qk", i + 1, k)
                k = yield from one("pv", i, k)

        summed = {}

        def vector_bands(kind, i):
            if kind == "qk":
                ready, free = [("q_psum", i), ("c", i)], [("minus_max", i - 1), ("masked", 0)]
            else:
                ready, free = [("a_psum", i), ("vt", i)], [("attended", i - 1)]
            behind = None
            for b in DVE_BANDS + (None,):
                if b is not None:
                    k = yield product(kind, i, b, prod[:, PLACE[b][0]:], ready + [summed.get(PLACE[b][1])],
                                      (kind, i) if b == DVE_BANDS[-1] else None)
                if behind:
                    pb, pk = behind
                    summed[pb] = yield band_sum(kind, i, pb, prod[:, PLACE[pb][0]:], [pk] + free,
                                                (kind + "_sum", i, pb))
                behind = (b, k)

        def attention():
            for i in range(NG + 1):
                if i < NG:
                    yield from vector_bands("qk", i)
                    sums = [("qk_sum", i, b) for b in DVE_BANDS] + [("qk_top", i)]
                    s = s_sb[:]
                    corner = bass.AP(tensor=s.tensor, offset=s.offset + 1, ap=[
                        list(s.ap[0]), [2 * G * HEADS + 2, BANDS], [HEADS, G]])
                    k = yield Op(dve, sums, lambda e, corner=corner: e.memset(corner, MASKED), 0.08)
                    for q in range(TQ, HEADS - 2, 2):
                        late = s[:, q * G * HEADS:(q + 2) * G * HEADS] \
                            .rearrange("p (qg k) -> p qg k", k=HEADS)[:, :, q + 2:]
                        k = yield Op(dve, [("qk_top", i)], lambda e, late=late: e.memset(late, MASKED), 0.08)
                    yield Op(dve, [k, ("minus_max", i - 2)], lambda e, i=i: e.tensor_reduce(
                        rowmax[:, i % 2, :], s_sb[:].rearrange("p (qg k) -> p qg k", k=HEADS), AX_X, ALU.max),
                        dve_us(G * D), ("max", i))
                if i > 0:
                    j = i - 1
                    yield Op(dve, [("a", j), ("attended", j - 2)], lambda e, j=j: e.tensor_reduce(
                        rowsum[:, j % 2, :], a_sb[:, j % 2, :].rearrange("p (qg k) -> p qg k", k=HEADS),
                        AX_X, ALU.add), dve_us(G * D), ("sum", j))
                    yield from vector_bands("pv", j)
                    yield Op(dve, [("sum", j)], lambda e, j=j: e.reciprocal(
                        rowsum[:, j % 2, :], rowsum[:, j % 2, :]), 0.27, ("inverse", j))

        def softmax():
            for i in range(NG):
                st = s_sb[:].rearrange("p (qg k) -> p qg k", k=HEADS)
                mx = rowmax[:, i % 2, :].unsqueeze(2).to_broadcast([P, HEADS * G, HEADS])
                dt = d_sb[:].rearrange("p (qg k) -> p qg k", k=HEADS)
                yield Op(pool, [("max", i), ("a", i - 1), ("a_psum", i - 1)],
                         lambda e, st=st, mx=mx, dt=dt: e.tensor_tensor(dt, st, mx, ALU.subtract),
                         pool_us(G * D), ("minus_max", i))
                yield Op(act, [("minus_max", i), ("pv_pool", i - 2), ("sum", i - 2)],
                         lambda e, i=i: e.activation(a_sb[:, i % 2, :], d_sb[:], ACT.Exp, scale=SCALE),
                         act_us(G * D), ("a", i))
                yield Op(act, [("minus_max", i), ("pv", i - 1)],
                         lambda e: e.activation(a_ps[:], d_sb[:], ACT.Exp, scale=SCALE),
                         act_us(G * D), ("a_psum", i))

        def residual(i):
            r = i % 2
            o = o_sb[:].rearrange("p (qg d) -> p qg d", d=HD)
            inv = rowsum[:, r, :].unsqueeze(2).to_broadcast([P, HEADS * G, HD])
            k = yield Op(pool, [("inverse", i), ("pv_top", i)] + [("pv_sum", i, b) for b in DVE_BANDS],
                         lambda e: e.tensor_tensor(o, o, inv, ALU.mult), pool_us(G * D))
            for g in range(G):
                xo = x_sb[:, i % XR, g * D:(g + 1) * D].rearrange("p (q d) -> p q d", q=HEADS)
                oo = o_sb[:].rearrange("p (q g d) -> p g q d", q=HEADS, g=G)[:, g]
                po = pay[:, r, g, 0:D].rearrange("p (q d) -> p q d", q=HEADS)
                yield Op(pool, [k, ("scatter", i - 2), ("q", i), ("q_psum", i)],
                         lambda e, xo=xo, oo=oo, po=po: e.tensor_tensor(po, xo, oo, ALU.add),
                         pool_us(D), ("x1", i) if g == G - 1 else None)
            M["attended", i] = M["x1", i]

        def row_tails(i):
            r = i % 2
            yield Op(pool, [("scatter", i - 2)], lambda e: e.iota(
                pay[:, r, :, :].bitcast(I32)[:, :, D + 2], pattern=[[1, G]], base=i * P * G, channel_multiplier=G),
                0.08, ("ids", i))
            yield Op(pool, [("scatter", i - 2)], lambda e: e.memset(pay[:, r, :, D + 3], 0.0), 0.04, ("pad", i))

        def gate(i):
            r = i % 2
            st = stat1[:, r]
            k = yield from ln_stats(lambda g: pay[:, r, g, 0:D], st, lambda g: xn1[:, g * D:(g + 1) * D],
                                    [("x1", i), ("logits", i - 1)])
            k = yield Op(pool, [k, ("minus_half", 0)], lambda e: e.tensor_tensor(
                pay[:, r, :, D + 1], st[:, 1, :], minus_half[:], ALU.pow), 0.63)
            shift = yield Op(pool, [k], lambda e: e.tensor_tensor(
                pay[:, r, :, D], st[:, 0, :], pay[:, r, :, D + 1], ALU.mult), 0.15, ("ln1_shift", i))
            for g in range(G):
                k = yield Op(act, [shift, ("logits", i - 1)], lambda e, g=g: e.activation(
                    xn1[:, g * D:(g + 1) * D], pay[:, r, g, 0:D], ACT.Identity,
                    scale=pay[:, r, g, D + 1:D + 2], bias=pay[:, r, g, D:D + 1]), act_us(D) + 0.1, ("xn1", i))
            for n in range(G * KD):
                k2 = yield Op(pe, [k, ("ident", 0), ("slots", i - 1),
                                     ("pick", picks_after(i - 1) - 1)], lambda e, n=n: e.transpose(
                    r_ps[:, n * P:(n + 1) * P], xn1[:, n * P:(n + 1) * P], ident[:]), 0.21)
            k = yield Op(act, [k2], lambda e: e.copy(xn1[:], r_ps[:]), act_us(G * D))
            for g in range(G):
                o = LG[:, g * E:(g + 1) * E]
                for k_ in range(KD):
                    n = g * KD + k_
                    yield Op(pe, [k, ("gate", 0)], lambda e, n=n, k_=k_, o=o: e.matmul(
                        o, xn1[:, n * P:(n + 1) * P], gate_sb[:, k_, :], start=(k_ == 0), stop=False), 0.43)
                yield Op(pe, [("tables", 0)], lambda e, o=o: e.matmul(
                    o, ones_row[:], gate_b_sb[:], start=False, stop=True), 0.43, ("logits", i) if g == G - 1 else None)

        def choose(i):
            v = [route[:, n, :].rearrange("p (g e) -> p g e", g=G) for n in range(6)]
            lg = LG.rearrange("p (g e) -> p g e", g=G)
            bc = lambda n: top[:, n, :].unsqueeze(2).to_broadcast([P, G, E])
            oh = onehot[:, i * G:(i + 1) * G, :]
            k = yield Op(dve, [("logits", i)], lambda e: e.tensor_reduce(top[:, 0, :], lg, AX_X, ALU.max), 0.08)
            k = yield Op(dve, [k], lambda e: e.tensor_tensor(v[0], lg, bc(0), ALU.is_ge), 0.08)
            k = yield Op(dve, [k, ("tables", 0)], lambda e: e.tensor_tensor(v[1], v[0], first_wins[:], ALU.mult), 0.08)
            k = yield Op(dve, [k], lambda e: e.tensor_reduce(top[:, 1, :], v[1], AX_X, ALU.max), 0.08)
            k = yield Op(dve, [k], lambda e: e.tensor_tensor(oh, v[1], bc(1), ALU.is_equal), 0.08, ("hot", i))
            for n in range(i * G, (i + 1) * G):
                k = yield Op(dve, [k], lambda e, n=n: e.tensor_tensor(
                    seen[:, n + 1, :], seen[:, n, :], onehot[:, n, :], ALU.add), 0.08,
                    ("seen", i) if n == (i + 1) * G - 1 else None)

        def rank(i):
            for g in range(G):
                n = i * G + g
                o = RK[:, g * E:(g + 1) * E]
                yield Op(pe, [("hot", i), ("before", 0)], lambda e, n=n, o=o: e.matmul(
                    o, before[:], onehot[:, n, :], start=True, stop=False), 0.06)
                yield Op(pe, [("seen", i)], lambda e, n=n, o=o: e.matmul(
                    o, ones_bf[:], seen[:, n, :], start=False, stop=True), 0.06)
            yield Op(pe, [], lambda e: e.matmul(CN, ones_bf[:], seen[:, (i + 1) * G, :], start=True, stop=True),
                     0.06, ("ranked", i))

        def scatter(i):
            r = i % 2
            v = [route[:, n, :].rearrange("p (g e) -> p g e", g=G) for n in range(6)]
            rk = RK.rearrange("p (g e) -> p g e", g=G)
            k = yield Op(dve, [("ranked", i)], lambda e: e.tensor_tensor(v[2], rk, region[:], ALU.add), 0.08)
            k = yield Op(dve, [k], lambda e: e.tensor_tensor(
                v[3], v[2], onehot[:, i * G:(i + 1) * G, :], ALU.mult), 0.08)
            k = yield Op(dve, [k], lambda e: e.tensor_reduce(slot_f[:], v[3], AX_X, ALU.add), 0.08)
            k = yield Op(dve, [k, ("scatter", i - 2)], lambda e: e.tensor_copy(slot_i[:, r, :], slot_f[:]),
                         0.08, ("slots", i))
            for g in range(G):
                yield Op(pool, [k, ("ids", i), ("pad", i), ("ln1_shift", i), ("x1", i)],
                         lambda e, g=g: e.indirect_dma_start(
                             out=sorted_rows, out_offset=bass.IndirectOffsetOnAxis(ap=slot_i[:, r, g:g + 1], axis=0),
                             in_=pay[:, r, g, :], in_offset=None, bounds_check=E * STRIDE - 1, oob_is_err=False),
                         1.04, ("scatter", i) if g == G - 1 else None, (s_scatter[r], 16 * G * (i // 2 + 1)), 130)

        def picks_after(i):
            n = (i + 1) * G * P - E * (P - 1)
            return NTILES if i == NG - 1 else max(0, (n - 1) // P + 1)

        group_of = {}
        for i in range(NG):
            for j in range(picks_after(i - 1), picks_after(i)):
                group_of[j] = i

        def pick(j, i):
            k = yield Op(dve, [("ranked", i), ("tables", 0), ("pick", j - 1), ("plan", j - 1)],
                         lambda e: e.tensor_tensor_reduce(
                             left[:], CN[0:1, :], used[:], 1.0, -1e9, ALU.add, ALU.max, pick_v[:, 0:1]), 0.09)
            k = yield Op(dve, [k], lambda e: e.tensor_scalar(
                pick_hot[:], left[:], pick_v[:, 0:1], None, ALU.is_equal), 0.13)
            k = yield Op(dve, [k], lambda e: e.tensor_tensor_reduce(
                left[:], pick_hot[:], used[:], 1.0, 0.0, ALU.mult, ALU.add, pick_v[:, 1:2]), 0.09)
            yield Op(dve, [k], lambda e: e.tensor_scalar(
                plan[:, j:j + 1], pick_v[:, 1:2], -float(E), float(E - 1), ALU.mult, ALU.add), 0.07, ("plan", j))
            yield Op(dve, [k], lambda e: e.scalar_tensor_tensor(
                out=used[:], in0=pick_hot[:], scalar=-float(P), in1=used[:], op0=ALU.mult, op1=ALU.add),
                0.08, ("pick", j))

        def fill():
            filler = prod[:, 0:2 * ROW].rearrange("p (r c) -> p r c", r=2)
            k = yield Op(dve, [("ranked", NG - 1)], lambda e: e.tensor_copy(count_i[:], CN[0:1, :]), 0.08)
            k2 = yield Op(pool, [("pv_sum", NG - 1, b) for b in DVE_BANDS],
                          lambda e: e.memset(filler, 0.0), 0.6)
            k2 = yield Op(pool, [k2], lambda e: e.memset(filler.bitcast(I32)[:, :, D + 2], SKIPPED_ROW), 0.1)
            for n in range(E):
                def issue(eng, n=n):
                    count = eng.value_load(count_i[0:1, n:n + 1], min_val=0, max_val=T)
                    row = nc.snap(count + n * STRIDE, min_val=0, max_val=E * STRIDE - 2 * P)
                    return eng.dma_start(
                        sorted_rows[bass.ds(row, 2 * P), :].rearrange("(p r) c -> p r c", r=2), filler)
                yield Op(sp, [k, k2], issue, 0.6, ("filled", 0), (s_fill, 16 * E), 260)

        def residuals():
            for i in range(NG):
                yield from residual(i)
                yield from row_tails(i)

        def gates():
            for i in range(NG):
                yield from gate(i)

        def routing():
            for i in range(NG):
                yield from choose(i)
                yield from rank(i)
                yield from scatter(i)

        def picks():
            for i in range(NG):
                for j in range(picks_after(i - 1), picks_after(i)):
                    yield from pick(j, i)

        def fetch():
            for j in range(NTILES):
                r, i = j % FR, group_of[j]
                waits = [("plan", j), ("scatter", i), ("scatter", i - 1), ("stored", j - FR)]
                if i == NG - 1:
                    waits.append(("filled", 0))

                def issue_rows(eng, j=j, r=r):
                    u = eng.value_load(plan[0:1, j:j + 1], min_val=0, max_val=E * (T + P))
                    row = nc.snap((u & (E - 1)) * STRIDE + (u >> (E.bit_length() - 1)),
                                  min_val=0, max_val=E * STRIDE - P)
                    return eng.dma_start(rows[:, r, :], sorted_rows[bass.ds(row, P), :])

                def issue_bias(eng, j=j, r=r):
                    u = eng.value_load(plan[0:1, j:j + 1], min_val=0, max_val=E * (T + P))
                    e_ = nc.snap(u & (E - 1), min_val=0, max_val=E - 1)
                    return eng.dma_start(brow[:, j % 2, :].unsqueeze(1), bias_rows[bass.ds(e_, 1), :, :]
                                         .rearrange("e r w -> r e w"))
                yield Op(sp, waits, issue_rows, 0.7, ("rows", j), (s_rows[r], 16 * (j // FR + 1)), 130)
                yield Op(sp, [("plan", j), ("bias_rows", 0), ("up", j - 2), ("down_bias", j - 2)], issue_bias, 0.6,
                         ("brow", j), (s_brow[j % 2], 16 * (j // 2 + 1)), 8)

        def expert_inputs():
            for j in range(NTILES):
                r = j % FR
                k = yield Op(act, [("rows", j), ("expert_t", j - 1)], lambda e, r=r: e.activation(
                    xn2[:], rows[:, r, 0:D], ACT.Identity, scale=rows[:, r, D + 1:D + 2], bias=rows[:, r, D:D + 1]),
                    act_us(D) + 0.1)
                for k_ in range(KD):
                    k2 = yield Op(pe, [k, ("xt_lo", j - 1), ("ident", 0)], lambda e, k_=k_: e.transpose(
                        xt2_ps[:, k_ * P:(k_ + 1) * P], xn2[:, k_ * P:(k_ + 1) * P], ident[:]),
                        0.21, ("expert_t", j) if k_ == KD - 1 else None)
                k = yield Op(act, [k2, ("up", j - 1)], lambda e: e.copy(xt_hi[:], xt2_ps), act_us(D), ("xt_hi", j))
                yield Op(dve, [k, ("up", j - 1)], lambda e: e.tensor_tensor(
                    xt_lo[:], xt2_ps, xt_hi[:], ALU.subtract), dve_us(D), ("xt_lo", j))

        weights_at = {}

        def up(j):
            def first(eng):
                u = eng.value_load(plan[0:1, j:j + 1], min_val=0, max_val=E * (T + P))
                weights_at[j] = nc.snap((u & (E - 1)) * (KD * H), min_val=0, max_val=(E - 1) * KD * H)
                return eng.matmul(h_ps[0][:, 0:P], brow[:, j % 2, 0:P], block_sum[:, 0, :], start=True, stop=False)
            for n in range(KH):
                c, at = n * P // HALF, n * P % HALF
                o = h_ps[c][:, at:at + P]
                if n == 0:
                    yield Op(pe, [("xt_lo", j), ("xt_hi", j), ("brow", j), ("weights", 0), ("weights", 1), ("plan", j), ("block_sum", 0),
                                  ("h_lo", j - 1, 0)], first, 0.3)
                else:
                    yield Op(pe, [("h_lo", j - 1, c)], lambda e, o=o, c=c, at=at: e.matmul(
                        o, brow[:, j % 2, at:at + P], block_sum[:, c, :], start=True, stop=False), pe_us(P))
                for k_ in range(KD):
                    for w, xt in ((w1_hi, xt_hi), (w1_hi, xt_lo), (w1_lo, xt_hi)):
                        last = k_ == KD - 1 and w is w1_lo
                        name = ("up_part", j, c) if last and (n + 1) * P % HALF == 0 else None
                        k = yield Op(pe, [], lambda e, o=o, n=n, k_=k_, w=w, xt=xt, last=last: e.matmul(
                            o, w[:, bass.ds(weights_at[j] + (k_ * H + n * P), P)],
                            xt[:, k_ * P:(k_ + 1) * P], start=False, stop=last), pe_us(P), name)
            M["up", j] = k

        def down(j):
            yield Op(pe, [("y", j - 1), ("h_lo", j, 0)], lambda e: e.matmul(
                y_ps, block_sum[:, BLOCKS - 1, :], brow[:, j % 2, 0:D], start=True, stop=False), pe_us(D), ("down_bias", j))
            for n in range(KH):
                for h, w in ((h_hi, w2_hi), (h_hi, w2_lo), (h_lo, w2_hi)):
                    last = n == KH - 1 and h is h_lo
                    yield Op(pe, [("h_lo", j, n * P // HALF)], lambda e, n=n, h=h, w=w, last=last: e.matmul(
                        y_ps, h[j % 2][:, n * P:(n + 1) * P], w[:, bass.ds(weights_at[j] + n * D, D)],
                        start=False, stop=last), pe_us(D), ("down", j) if last else None)

        def ups():
            for j in range(NTILES):
                yield from up(j)

        def downs():
            for j in range(NTILES):
                yield from down(j)

        def relus():
            for j in range(NTILES):
                for c in range(H // HALF):
                    cols = slice(c * HALF, (c + 1) * HALF)
                    k = yield Op(act, [("up_part", j, c), ("down", j - 2), ("weights", 0), ("weights", 1)],
                                 lambda e, j=j, c=c, cols=cols: e.activation(h_hi[j % 2][:, cols], h_ps[c][:], ACT.Relu),
                                 act_us(HALF))
                    yield Op(dve, [k, ("down", j - 2)], lambda e, j=j, c=c, cols=cols: e.scalar_tensor_tensor(
                        out=h_lo[j % 2][:, cols], in0=h_ps[c][:], scalar=0.0, in1=h_hi[j % 2][:, cols],
                        op0=ALU.max, op1=ALU.subtract), dve_us(HALF), ("h_lo", j, c))

        def results():
            for j in range(NTILES):
                r = j % FR
                k = yield Op(dve, [("down", j)], lambda e, r=r: e.scalar_tensor_tensor(
                    out=rows[:, r, 0:D], in0=y_ps, scalar=1.0 / (W_SCALE * W_SCALE), in1=rows[:, r, 0:D],
                    op0=ALU.mult, op1=ALU.add), dve_us(D), ("y", j))
                yield Op(pool, [k], lambda e, r=r: e.indirect_dma_start(
                    out=out, out_offset=bass.IndirectOffsetOnAxis(
                        ap=rows[:, r, :].bitcast(I32)[:, D + 2:D + 3], axis=0),
                    in_=rows[:, r, 0:D], in_offset=None, bounds_check=T - 1, oob_is_err=False),
                    1.04, ("stored", j), (s_out[r], 16 * (j // FR + 1)), 128)

        order = Order()
        M = order.marks
        order.merge([
            (0.0, load_x()), (4.0, load_context()), (0, small_constants()), (-0.3, small_inputs()),
            (-0.3, fill()), (-0.6, residuals()), (0, gates()), (0, routing()), (0, picks()), (-0.6, fetch()), (-0.3, results()), (0, expert_inputs()), (0, relus()),
            (0.3, downs()), (0.3, ups()), (-0.3, softmax()), (0, x_stats()),
            (0.15, queries(q_ps[:], "q_psum", lambda i: [("qk", i - 1)])),
            (0, queries(q_sb[:], "q", lambda i: [("qk_pool", i - 1)])),
            (-0.6, turned_values()), (0, top_products()), (0.15, top_sums()), (0.15, attention()), (-0.3, weights()),
        ])

        block = stack.enter_context(nc.Block())

        @block.sync
        def _(eng):
            sp.run(eng)
            for r in range(FR):
                eng.wait_ge(s_out[r], 16 * ((NTILES - r + FR - 1) // FR))

        @block.scalar
        def _(eng):
            act.run(eng)

        @block.vector
        def _(eng):
            dve.run(eng)

        @block.gpsimd
        def _(eng):
            pool.run(eng)

        @block.tensor
        def _(eng):
            pe.run(eng)


def kernel(x, ctx_1024, L0_ffn_gate_w, L0_ffn_gate_b, L0_ffn_w1, L0_ffn_b1, L0_ffn_w2, L0_ffn_b2):
    import concourse.bacc as bacc
    from concourse.bass_utils import run_bass_kernel_spmd

    B, S, D = x.shape
    E, H, _ = L0_ffn_w1.shape
    lay = np.ascontiguousarray
    arrays = {
        "x": lay(x).reshape(B * S, D),
        "ctx": lay(ctx_1024).reshape(B * S, D),
        "gate_w": lay(np.transpose(np.reshape(L0_ffn_gate_w, (E, D // P, P)), (2, 1, 0))),
        "gate_b": lay(np.reshape(L0_ffn_gate_b, (1, E))),
        "w1": lay(np.transpose(np.reshape(L0_ffn_w1, (E, H, D // P, P)), (3, 0, 2, 1))).reshape(P, E, (D // P) * H),
        "b1": lay(L0_ffn_b1),
        "w2": lay(np.transpose(np.reshape(L0_ffn_w2, (E, D, H // P, P)), (3, 0, 2, 1))).reshape(P, E, (H // P) * D),
        "b2": lay(L0_ffn_b2),
    }
    nc = bacc.Bacc("TRN2", target_bir_lowering=False, num_devices=1)
    args = [nc.dram_tensor(n, a.shape, mybir.dt.from_np(a.dtype), kind="ExternalInput").ap() for n, a in arrays.items()]
    res = nc.dram_tensor("result", (B * S, D), F32, kind="ExternalOutput").ap()
    xattn_moe_kernel(nc, *args, res)
    got = run_bass_kernel_spmd(nc, [arrays], core_ids=[0])
    return got.results[0]["result"].reshape(B, S, D)
```

```python
from contextlib import ExitStack

import numpy as np

import concourse.bass as bass
from concourse import mybir

F32 = mybir.dt.float32
F16 = mybir.dt.float16
BF16 = mybir.dt.bfloat16
I32 = mybir.dt.int32
ALU = mybir.AluOpType
ACT = mybir.ActivationFunctionType
AX_X = mybir.AxisListType.X

P = 128
HEADS = 16
EPS = 1e-5
MASKED = -4e18
W_SCALE = 64.0
G = 2
SKIPPED_ROW = 1 << 20


class Mark:

    def __init__(self, sem, value, at):
        self.sem, self.value, self.at = sem, value, at


class Queue:

    def __init__(self, sem):
        self.sem, self.steps, self.count, self.free, self.issued = sem, [], 0, 0.0, 0.0

    def run(self, engine):
        waited = {}
        for marks, issue, sem, inc in self.steps:
            for m in marks:
                if waited.get(m.sem, 0) < m.value:
                    engine.wait_ge(m.sem, m.value)
                    waited[m.sem] = m.value
            issue(engine).then_inc(sem, inc)


class Op:

    def __init__(self, queue, waits, issue, us, name=None, dma=None, kbytes=0, address=0.0):
        self.queue, self.waits, self.issue, self.us, self.name = queue, waits, issue, us, name
        self.dma, self.kbytes, self.address = dma, kbytes, address


class Order:

    WAKE = 0.13
    AHEAD = 0.25

    def __init__(self):
        self.marks, self.dma_free = {}, 0.0

    def start(self, op):
        q = op.queue
        at = max(q.free, max(q.issued, q.free - self.AHEAD) + op.address)
        for w in op.waits:
            if w is None:
                continue
            if not isinstance(w, Mark):
                if w[1] < 0:
                    continue
                if w not in self.marks:
                    return None
                w = self.marks[w]
            at = max(at, w.at + self.WAKE)
        return at

    def commit(self, op, at):
        marks = [w if isinstance(w, Mark) else self.marks[w] for w in op.waits
                 if w is not None and (isinstance(w, Mark) or w[1] >= 0)]
        q = op.queue
        q.issued = max(q.issued, q.free - self.AHEAD) + op.address
        q.free = at + op.us
        if op.dma:
            sem, value = op.dma
            q.steps.append((marks, op.issue, sem, 16))
            self.dma_free = max(self.dma_free, q.free + 0.8) + op.kbytes / 350.0
            m = Mark(sem, value, self.dma_free + 1.7)
        else:
            q.count += 1
            q.steps.append((marks, op.issue, q.sem, 1))
            m = Mark(q.sem, q.count, q.free)
        if op.name:
            self.marks[op.name] = m
        return m

    def merge(self, lanes):
        backs, lanes = zip(*lanes)
        wanted = [next(lane, None) for lane in lanes]
        while any(wanted):
            ready = [(self.start(op), n) for n, op in enumerate(wanted) if op is not None]
            ready = [(at + backs[n], n, at) for at, n in ready if at is not None]
            if not ready:
                raise RuntimeError(f"every lane waits: {[(n, o.name, o.waits) for n, o in enumerate(wanted) if o]}")
            _, n, at = min(ready)
            m = self.commit(wanted[n], at)
            try:
                wanted[n] = lanes[n].send(m)
            except StopIteration:
                wanted[n] = None


def xattn_moe_kernel(nc, x, ctx_in, gate_w, gate_b, w1, b1, w2, b2, out):
    T, D = x.shape
    E = gate_b.shape[0]
    H = w1.shape[2] * P // D
    HD = D // HEADS
    KD, KH = D // P, H // P
    NT = T // P
    NG = NT // G
    BANDS = HEADS // 2
    NTILES = NT + E - 1
    STRIDE = T + 2 * P
    ROW = D + 4
    HALF = 512
    SCALE = 1.0 / float(np.sqrt(HD))
    WC = H
    CHUNKS = 2 * E * KD * H // WC
    assert KD * H == KH * D

    dve_us = lambda n: 0.065 + n / 960
    act_us = lambda n: 0.21 + n / 1200
    pool_us = lambda n: 0.1 + n * 0.0021
    pe_us = lambda n: max(n, 64) / 2400 + 0.003
    pe32_us = lambda n: max(0.213, 4 * n / 2400)

    def band_size(b):
        return 2 * G * (2 * b + 2) * HD

    sorted_rows = nc.dram_tensor("sorted_rows", [E * STRIDE, ROW], F32).ap()
    BLOCKS = H // HALF + 1
    bias_rows = nc.dram_tensor("bias_rows", [E, BLOCKS * 3, HALF], BF16).ap()

    stack = ExitStack()
    with stack:
        def sb(name, shape, dt=F32):
            return stack.enter_context(nc.sbuf_tensor(name, shape, dt))

        def ps(name):
            return stack.enter_context(nc.psum_tensor(name, [P, HALF], F32))

        def sem(name):
            return stack.enter_context(nc.semaphore(name))

        ident = sb("ident", [P, P])
        minus_scaled = sb("minus_scaled", [P, P], F16)
        before = sb("before", [P, P], BF16)
        ones_bf = sb("ones_bf", [P, P], BF16)
        minus_half = sb("minus_half", [P, G])
        first_wins = sb("first_wins", [P, G, E])
        region = sb("region", [P, G, E])
        gate_sb = sb("gate_sb", [P, KD, E])
        gate_b_sb = sb("gate_b_sb", [E, 1])
        w1_hi, w1_lo, w2_hi, w2_lo = [sb(n, [P, E * KD * H], F16) for n in ("w1_hi", "w1_lo", "w2_hi", "w2_lo")]
        XR = 4
        x_sb = sb("x_sb", [P, XR, G * D])
        c_sb = sb("c_sb", [P, 2, G * D])
        vt_sb = sb("vt_sb", [P, 2, G * D])
        q_sb = sb("q_sb", [P, G * D])
        a_sb = sb("a_sb", [P, 2, G * D])
        s_sb = sb("s_sb", [P, G * D])
        d_sb = sb("d_sb", [P, G * D])
        o_sb = sb("o_sb", [P, G * D])
        DVE_BANDS = (5, 0, 4, 1, 3, 2)
        PLACE = {5: (0, 3), 0: (768, 2), 4: (896, 2), 1: (0, 5), 3: (256, 5), 2: (768, 4)}
        TOP = 4
        TQ = HEADS - TOP
        TC = TOP * G * HEADS
        prod = sb("prod", [P, max(at + band_size(b) for b, (at, _) in PLACE.items())])
        pprod = sb("pprod", [P, 2, TC * HD])
        passed = sb("passed", [P, G, D], BF16)
        xstat = sb("xstat", [P, 2, 4, G])
        rowmax = sb("rowmax", [P, 2, HEADS * G])
        rowsum = sb("rowsum", [P, 2, HEADS * G])
        pay = sb("pay", [P, 2, G, ROW])
        stat1 = sb("stat1", [P, 2, 4, G])
        xn1 = sb("xn1", [P, G * D])
        route = sb("route", [P, 6, G * E])
        top = sb("top", [P, 2, G])
        onehot = sb("onehot", [P, NT, E], BF16)
        seen = sb("seen", [P, NT + 1, E], BF16)
        slot_f = sb("slot_f", [P, G])
        slot_i = sb("slot_i", [P, 2, G], I32)
        used = sb("used", [1, E])
        left = sb("left", [1, E])
        pick_hot = sb("pick_hot", [1, E])
        pick_v = sb("pick_v", [1, 4])
        plan = sb("plan", [1, NTILES], I32)
        count_i = sb("count_i", [1, E], I32)
        SHARED = 4
        shifts = sb("shifts", [1, SHARED], I32)
        experts_of = sb("experts_of", [1, SHARED], I32)
        digits = sb("digits", [1, SHARED])
        packed_f = sb("packed_f", [1, 1])
        packed = sb("packed", [1, NTILES], I32)
        FR = 4
        rows = sb("rows", [P, FR, ROW])
        brow = sb("brow", [BLOCKS * 3, 2, HALF], BF16)
        block_sum = sb("block_sum", [BLOCKS * 3, BLOCKS, P], BF16)
        xn2 = sb("xn2", [P, D])
        xt_hi = sb("xt_hi", [P, 2, D], F16)
        xt_lo = sb("xt_lo", [P, 2, D], F16)
        h_parts = sb("h_parts", [P, 2 * 2 * H], F16)
        h_hi = [h_parts[:, n * 2 * H:n * 2 * H + H] for n in range(2)]
        h_lo = [h_parts[:, n * 2 * H + H:(n + 1) * 2 * H] for n in range(2)]
        w_in = [h_parts[:, n * 2 * WC:(n + 1) * 2 * WC].bitcast(F32) for n in range(2)]

        q_ps, a_ps, r_ps, m_ps, h0_ps, h1_ps, y_bank, top_ps = [ps(n) for n in
            ("q_ps", "a_ps", "r_ps", "m_ps", "h0_ps", "h1_ps", "y_ps", "top_ps")]
        h_ps = (h0_ps, h1_ps)
        xt2_ps, y_ps = m_ps[:, 0:D], y_bank[:, 0:D]
        LG = r_ps[:, 0:G * E]
        RK = r_ps[:, G * E:2 * G * E]
        CN = r_ps[:, 2 * G * E:2 * G * E + E]

        pe, act, dve, pool, sp = [Queue(sem(n)) for n in ("s_pe", "s_act", "s_dve", "s_pool", "s_sp")]
        s_x = [sem(f"s_x{n}") for n in range(XR)]
        s_c = [sem(f"s_c{n}") for n in range(2)]
        s_w = [sem(f"s_w{n}") for n in range(2)]
        s_gate, s_bias_in, s_bias_out, s_fill = [sem(n) for n in ("s_gate", "s_bias_in", "s_bias_out", "s_fill")]
        s_scatter = [sem(f"s_scatter{n}") for n in range(2)]
        s_rows = [sem(f"s_rows{n}") for n in range(FR)]
        s_brow = [sem(f"s_brow{n}") for n in range(2)]
        s_out = [sem(f"s_out{n}") for n in range(FR)]

        x_v = x.rearrange("(i p g) d -> i p (g d)", p=P, g=G)
        c_v = ctx_in.rearrange("(i p g) d -> i p (g d)", p=P, g=G)
        KB_GROUP = P * G * D * 4 / 1024

        def load_x():
            for i in range(NG):
                r = i % XR
                yield Op(sp, [("x1", i - XR)], lambda e, i=i, r=r: e.dma_start(x_sb[:, r, :], x_v[i]),
                         0.5, ("x", i), (s_x[r], 16 * (i // XR + 1)), KB_GROUP)

        def load_context():
            for i in range(NG):
                c = i % 2
                yield Op(sp, [("qk", i - 2), ("qk_pool", i - 2), ("vt", i - 2)],
                         lambda e, i=i, c=c: e.dma_start(c_sb[:, c, :], c_v[i]),
                         0.5, ("c", i), (s_c[c], 16 * (i // 2 + 1)), KB_GROUP)

        def weights():
            def load(n):
                src = (w1, w2)[n % 2].rearrange("p e w -> p (e w)")[:, n // 2 * WC:(n // 2 + 1) * WC]
                return Op(sp, [("weight_lo", n - 2, WC // HALF - 1)], lambda e: e.dma_start(w_in[n % 2], src),
                          0.5, ("weight_in", n), (s_w[n % 2], 16 * (n // 2 + 1)), P * WC * 4 / 1024)
            yield load(0)
            yield load(1)
            for n in range(CHUNKS):
                at = n // 2 * WC
                hi, lo = ((w1_hi, w1_lo), (w2_hi, w2_lo))[n % 2]
                high = yield Op(act, [("weight_in", n)], lambda e, n=n, hi=hi, at=at: e.activation(
                    hi[:, at:at + WC], w_in[n % 2], ACT.Copy, scale=W_SCALE), act_us(WC))
                if n % 2:
                    yield Op(dve, [high], lambda e, n=n, hi=hi, lo=lo, at=at: e.scalar_tensor_tensor(
                        out=lo[:, at:at + WC], in0=w_in[n % 2], scalar=W_SCALE, in1=hi[:, at:at + WC],
                        op0=ALU.mult, op1=ALU.subtract), dve_us(WC), ("weight_lo", n, WC // HALF - 1))
                    if n + 2 < CHUNKS:
                        yield load(n + 2)
                    continue
                for c in range(WC // HALF):
                    cols = slice(at + c * HALF, at + (c + 1) * HALF)
                    yield Op(pe, [("weight_in", n), ("weight_lo", n - 2, c), ("ident", 0)],
                             lambda e, n=n, c=c: e.matmul(
                                 h_ps[c][:], ident[:], w_in[n % 2][:, c * HALF:(c + 1) * HALF],
                                 start=True, stop=False), pe32_us(HALF))
                    k = yield Op(pe, [high, ("minus_scaled", 0)], lambda e, c=c, hi=hi, cols=cols: e.matmul(
                        h_ps[c][:], minus_scaled[:], hi[:, cols], start=False, stop=True), pe_us(HALF))
                    yield Op(act, [k], lambda e, c=c, lo=lo, cols=cols: e.activation(
                        lo[:, cols], h_ps[c][:], ACT.Copy, scale=W_SCALE), act_us(HALF), ("weight_lo", n, c))
                if n + 2 < CHUNKS:
                    yield load(n + 2)
            M["weights", 0] = M["weight_lo", CHUNKS - 1, WC // HALF - 1]
            M["weights", 1] = M["weight_lo", CHUNKS - 2, WC // HALF - 1]

        def small_constants():
            k = yield Op(pool, [], lambda e: e.memset(ident[:], 1.0), 0.2)
            yield Op(pool, [k], lambda e: e.affine_select(
                out=ident[:], in_=ident[:], compare_op=ALU.is_equal, fill=0.0, base=0,
                pattern=[[-1, P]], channel_multiplier=1), 0.25, ("ident", 0))
            yield Op(pool, [("ident", 0)], lambda e: e.tensor_scalar(
                minus_scaled[:], ident[:], -1.0 / W_SCALE, 0.0, ALU.mult, ALU.add), 0.25, ("minus_scaled", 0))
            k = yield Op(pool, [], lambda e: e.memset(ones_bf[:], 1.0), 0.2)
            yield Op(pool, [k], lambda e: e.affine_select(
                out=before[:], in_=ones_bf[:], compare_op=ALU.is_gt, fill=0.0, base=0,
                pattern=[[1, P]], channel_multiplier=-1), 0.25, ("before", 0))
            yield Op(pool, [], lambda e: e.memset(minus_half[:], -0.5), 0.1, ("minus_half", 0))
            k = yield Op(pool, [], lambda e: e.memset(block_sum[:], 1.0), 0.3)
            k = yield Op(pool, [k], lambda e: e.affine_select(
                out=block_sum[:], in_=block_sum[:], compare_op=ALU.is_ge, fill=0.0, base=0,
                pattern=[[-3, BLOCKS], [0, P]], channel_multiplier=1), 0.5)
            yield Op(pool, [k], lambda e: e.affine_select(
                out=block_sum[:], in_=block_sum[:], compare_op=ALU.is_ge, fill=0.0, base=2,
                pattern=[[3, BLOCKS], [0, P]], channel_multiplier=-1), 0.5, ("block_sum", 0))
            yield Op(dve, [], lambda e: e.memset(s_sb[:], MASKED), 0.6, ("masked", 0))
            yield Op(dve, [], lambda e: e.memset(seen[:, 0, :], 0.0), 0.1)
            for n in range(SHARED):
                yield Op(dve, [], lambda e, n=n: e.memset(shifts[:, n:n + 1], E ** n), 0.1)
            for n in range(E):
                yield Op(dve, [], lambda e, n=n: e.memset(first_wins[:, :, n], float(E - n)), 0.1)
                yield Op(dve, [], lambda e, n=n: e.memset(region[:, :, n], float(n * STRIDE)), 0.1)
                yield Op(dve, [], lambda e, n=n: e.memset(used[:, n:n + 1], float(E - 1 - n) / E), 0.1,
                         ("tables", 0) if n == E - 1 else None)

        BW = BLOCKS * HALF
        setup = pprod[0:E].rearrange("p a b -> p (a b)")
        bias_wide = setup[:, 0:BW]
        bias_parts = setup[:, BW:BW + 3 * BW // 2].bitcast(BF16).rearrange("p (n w) -> p n w", n=3)

        def small_inputs():
            z = yield Op(dve, [], lambda e: e.memset(bias_wide[:, H + D:], 0.0), 0.1)
            yield Op(sp, [], lambda e: e.dma_start(bias_wide[:, 0:H], b1), 0.5, None, (s_bias_in, 32), 32)
            k = yield Op(sp, [], lambda e: e.dma_start(bias_wide[:, H:H + D], b2), 0.5, None, (s_bias_in, 32), 8)
            yield Op(sp, [], lambda e: e.dma_start(gate_sb[:], gate_w), 0.5, None, (s_gate, 32), 8)
            yield Op(sp, [], lambda e: e.dma_start(gate_b_sb[:], gate_b), 0.5, ("gate", 0), (s_gate, 32), 1)
            us = dve_us(BW)
            k = yield Op(dve, [k], lambda e: e.tensor_scalar(
                bias_wide[:, 0:H], bias_wide[:, 0:H], W_SCALE, None, ALU.mult), us)
            k = yield Op(dve, [k], lambda e: e.tensor_scalar(
                bias_wide[:, H:H + D], bias_wide[:, H:H + D], W_SCALE * W_SCALE, None, ALU.mult), us)
            for n in range(3):
                k = yield Op(dve, [k], lambda e, n=n: e.tensor_copy(bias_parts[:, n, :], bias_wide), us)
                if n < 2:
                    k = yield Op(dve, [k], lambda e, n=n: e.tensor_tensor(
                        bias_wide, bias_wide, bias_parts[:, n, :], ALU.subtract), us)
            for n in range(3):
                yield Op(sp, [k], lambda e, n=n: e.dma_start(
                    bias_rows.rearrange("e (c n) w -> e c n w", n=3)[:, :, n, :],
                    bias_parts[:, n, :].rearrange("e (c w) -> e c w", c=BLOCKS)),
                         0.5, ("bias_rows", 0), (s_bias_out, 48), 8)

        def ln_stats(src, st, passed, waits, rstd, shift, name):
            for g in range(G):
                k = yield Op(act, waits, lambda e, g=g: e.activation(
                    passed(g), src(g), ACT.Identity, scale=-1.0 / D, accum_out=st[:, 0, g:g + 1]),
                    act_us(D) + 0.09)
            for g in range(G):
                k2 = yield Op(act, [k], lambda e, g=g: e.activation(
                    passed(g), src(g), ACT.Square, bias=st[:, 0, g:g + 1],
                    accum_out=st[:, 1, g:g + 1]), act_us(D) + 0.09)
            k = yield Op(pool, [k2], lambda e: e.tensor_scalar(
                st[:, 1, :], st[:, 1, :], 1.0 / D, EPS, ALU.mult, ALU.add), 0.16)
            k = yield Op(pool, [k, ("minus_half", 0)], lambda e: e.tensor_tensor(
                rstd, st[:, 1, :], minus_half[:], ALU.pow), 0.63)
            return (yield Op(pool, [k], lambda e: e.tensor_tensor(shift, st[:, 0, :], rstd, ALU.mult), 0.15, name))

        def x_stats():
            for i in range(NG):
                st = xstat[:, i % 2]
                x_g = lambda g, i=i: x_sb[:, i % XR, g * D:(g + 1) * D]
                yield from ln_stats(x_g, st, lambda g: passed[:, g],
                                    [("x", i), ("q_psum", i - 2), ("q", i - 2), ("q_shift", i - 1)],
                                    st[:, 2, :], st[:, 3, :], ("q_shift", i))

        def queries(dst, name, frees):
            for i in range(NG):
                st = xstat[:, i % 2]
                for g in range(G):
                    o = dst.rearrange("p (h g d) -> p g h d", h=HEADS, g=G)[:, g]
                    s = x_sb[:, i % XR, g * D:(g + 1) * D].rearrange("p (h d) -> p h d", h=HEADS)
                    yield Op(act, [("q_shift", i)] + frees(i), lambda e, g=g, o=o, s=s, st=st: e.activation(
                        o, s, ACT.Identity, scale=st[:, 2, g:g + 1], bias=st[:, 3, g:g + 1]),
                        act_us(D) + 0.1, (name, i) if g == G - 1 else None)

        def turned_values():
            for i in range(NG):
                v = c_sb[:, i % 2, :].rearrange("p (g k d) -> p g d k", g=G, k=HEADS)
                o = vt_sb[:, i % 2, :].rearrange("p (g d k) -> p g d k", g=G, k=HEADS)
                for g in range(G):
                    yield Op(act, [("c", i), ("pv", i - 2), ("pv_pool", i - 2)],
                             lambda e, g=g, o=o, v=v: e.copy(o[:, g], v[:, g]), act_us(D),
                             ("vt", i) if g == G - 1 else None)

        def qk_operands(b, q, c):
            K = 2 * b + 2
            q_ = q[:, 2 * b * G * HD:(2 * b + 2) * G * HD].rearrange("p (qg d) -> p qg d", d=HD)
            c_ = c.rearrange("p (g k d) -> p g (k d)", g=G, k=HEADS)[:, :, 0:K * HD]
            return (q_.unsqueeze(2).to_broadcast([P, 2 * G, K, HD]),
                    c_.unsqueeze(1).to_broadcast([P, 2, G, K * HD]))

        def pv_operands(b, a, v):
            K = 2 * b + 2
            a_ = a[:, 2 * b * G * HEADS:(2 * b + 2) * G * HEADS].rearrange("p (qg k) -> p qg k", k=HEADS)[:, :, 0:K]
            v_ = v.rearrange("p (gd k) -> p gd k", k=HEADS)[:, :, 0:K]
            return (a_.unsqueeze(2).to_broadcast([P, 2 * G, HD, K]),
                    v_.unsqueeze(1).to_broadcast([P, 2, G * HD, K]))

        def product(kind, i, b, dst, waits, name):
            n, K = band_size(b), 2 * b + 2
            if kind == "qk":
                in0, in1 = qk_operands(b, q_ps[:], c_sb[:, i % 2, :])
                o = dst[:, 0:n].rearrange("p (qg k d) -> p qg k d", qg=2 * G, k=K)
            else:
                in0, in1 = pv_operands(b, a_ps[:], vt_sb[:, i % 2, :])
                o = dst[:, 0:n].rearrange("p (qg d k) -> p qg d k", qg=2 * G, k=K)
            return Op(dve, waits, lambda e: e.tensor_tensor(o, in0, in1, ALU.mult), dve_us(n), name)

        def band_sum(kind, i, b, src, waits, name):
            n, K = band_size(b), 2 * b + 2
            if kind == "qk":
                o = s_sb[:, 2 * b * G * HEADS:(2 * b + 2) * G * HEADS] \
                    .rearrange("p (qg k) -> p qg k", k=HEADS)[:, :, 0:K]
                v = src[:, 0:n].rearrange("p (qg k d) -> p qg k d", k=K, d=HD)
            else:
                o = o_sb[:, 2 * b * G * HD:(2 * b + 2) * G * HD]
                v = src[:, 0:n].rearrange("p (qgd k) -> p qgd k", k=K)
            return Op(dve, waits, lambda e: e.tensor_reduce(o, v, AX_X, ALU.add), dve_us(n), name)

        def top_products():
            def one(kind, i):
                if kind == "qk":
                    ready, dst = [("q", i), ("c", i), ("bias_rows", 0)], pprod[:, 0, :]
                    fixed = q_sb[:, TQ * G * HD:].rearrange("p (q g d) -> p q g d", q=TOP, g=G)
                    moving = c_sb[:, i % 2, :].rearrange("p (g kd) -> p g kd", g=G)
                else:
                    ready, dst = [("a", i), ("vt", i), ("bias_rows", 0)], pprod[:, 1, :]
                    fixed = a_sb[:, i % 2, TQ * G * HEADS:].rearrange("p (q g k) -> p q g k", q=TOP, g=G)
                    moving = vt_sb[:, i % 2, :].rearrange("p (g dk) -> p g dk", g=G)
                o = dst.rearrange("p (qg m n) -> p qg m n", qg=TOP * G, m=HEADS)
                fixed = fixed.rearrange("p q g n -> p (q g) n").unsqueeze(2).to_broadcast([P, TOP * G, HEADS, HD])
                moving = moving.unsqueeze(1).to_broadcast([P, TOP, G, HEADS * HD])
                return Op(pool, ready + [(kind + "_top_added", i - 1)],
                          lambda e: e.tensor_tensor(o, fixed, moving, ALU.mult), pool_us(TC * HD), (kind + "_pool", i))
            yield one("qk", 0)
            for i in range(NG):
                if i + 1 < NG:
                    yield one("qk", i + 1)
                yield one("pv", i)

        def top_sums():
            def one(kind, i, bank_read):
                src = pprod[:, ("qk", "pv").index(kind), :].rearrange("p (c n) -> p c n", n=HD)
                acc = top_ps[:, ("qk", "pv").index(kind) * TC:][:, 0:TC]
                for n in range(HD):
                    yield Op(pe, [(kind + "_pool", i), bank_read, ("ident", 0)],
                             lambda e, n=n: e.matmul(acc, ident[:], src[:, :, n], start=n == 0, stop=n == HD - 1),
                             pe32_us(TC), (kind + "_top_added", i) if n == HD - 1 else None)
                free, dst = [(("minus_max", i - 1), s_sb), (("attended", i - 1), o_sb)][kind == "pv"]
                return (yield Op(act, [(kind + "_top_added", i), free, ("masked", 0)],
                                 lambda e: e.copy(dst[:, TQ * G * HEADS:], acc), act_us(TC), (kind + "_top", i)))
            k = yield from one("qk", 0, None)
            for i in range(NG):
                if i + 1 < NG:
                    k = yield from one("qk", i + 1, k)
                k = yield from one("pv", i, k)

        summed = {}

        def vector_bands(kind, i):
            if kind == "qk":
                ready, free = [("q_psum", i), ("c", i)], [("minus_max", i - 1), ("masked", 0)]
            else:
                ready, free = [("a_psum", i), ("vt", i)], [("attended", i - 1)]
            behind = None
            for b in DVE_BANDS + (None,):
                if b is not None:
                    k = yield product(kind, i, b, prod[:, PLACE[b][0]:], ready + [summed.get(PLACE[b][1])],
                                      (kind, i) if b == DVE_BANDS[-1] else None)
                if behind:
                    pb, pk = behind
                    summed[pb] = yield band_sum(kind, i, pb, prod[:, PLACE[pb][0]:], [pk] + free,
                                                (kind + "_sum", i, pb))
                behind = (b, k)

        def attention():
            for i in range(NG + 1):
                if i < NG:
                    yield from vector_bands("qk", i)
                    sums = [("qk_sum", i, b) for b in DVE_BANDS] + [("qk_top", i)]
                    s = s_sb[:]
                    corner = bass.AP(tensor=s.tensor, offset=s.offset + 1, ap=[
                        list(s.ap[0]), [2 * G * HEADS + 2, BANDS], [HEADS, G]])
                    k = yield Op(dve, sums, lambda e, corner=corner: e.memset(corner, MASKED), 0.08)
                    for q in range(TQ, HEADS - 2, 2):
                        late = s[:, q * G * HEADS:(q + 2) * G * HEADS] \
                            .rearrange("p (qg k) -> p qg k", k=HEADS)[:, :, q + 2:]
                        k = yield Op(dve, [("qk_top", i)], lambda e, late=late: e.memset(late, MASKED), 0.08)
                    yield Op(dve, [k, ("minus_max", i - 2)], lambda e, i=i: e.tensor_reduce(
                        rowmax[:, i % 2, :], s_sb[:].rearrange("p (qg k) -> p qg k", k=HEADS), AX_X, ALU.max),
                        dve_us(G * D), ("max", i))
                if i > 0:
                    j = i - 1
                    yield Op(dve, [("a", j), ("attended", j - 2)], lambda e, j=j: e.tensor_reduce(
                        rowsum[:, j % 2, :], a_sb[:, j % 2, :].rearrange("p (qg k) -> p qg k", k=HEADS),
                        AX_X, ALU.add), dve_us(G * D), ("sum", j))
                    yield from vector_bands("pv", j)
                    yield Op(dve, [("sum", j)], lambda e, j=j: e.reciprocal(
                        rowsum[:, j % 2, :], rowsum[:, j % 2, :]), 0.27, ("inverse", j))

        def softmax():
            for i in range(NG):
                st = s_sb[:].rearrange("p (qg k) -> p qg k", k=HEADS)
                mx = rowmax[:, i % 2, :].unsqueeze(2).to_broadcast([P, HEADS * G, HEADS])
                dt = d_sb[:].rearrange("p (qg k) -> p qg k", k=HEADS)
                yield Op(pool, [("max", i), ("a", i - 1), ("a_psum", i - 1)],
                         lambda e, st=st, mx=mx, dt=dt: e.tensor_tensor(dt, st, mx, ALU.subtract),
                         pool_us(G * D), ("minus_max", i))
                yield Op(act, [("minus_max", i), ("pv_pool", i - 2), ("sum", i - 2)],
                         lambda e, i=i: e.activation(a_sb[:, i % 2, :], d_sb[:], ACT.Exp, scale=SCALE),
                         act_us(G * D), ("a", i))
                yield Op(act, [("minus_max", i), ("pv", i - 1)],
                         lambda e: e.activation(a_ps[:], d_sb[:], ACT.Exp, scale=SCALE),
                         act_us(G * D), ("a_psum", i))

        def residual(i):
            r = i % 2
            o = o_sb[:].rearrange("p (qg d) -> p qg d", d=HD)
            inv = rowsum[:, r, :].unsqueeze(2).to_broadcast([P, HEADS * G, HD])
            k = yield Op(pool, [("inverse", i), ("pv_top", i)] + [("pv_sum", i, b) for b in DVE_BANDS],
                         lambda e: e.tensor_tensor(o, o, inv, ALU.mult), pool_us(G * D))
            for g in range(G):
                xo = x_sb[:, i % XR, g * D:(g + 1) * D].rearrange("p (q d) -> p q d", q=HEADS)
                oo = o_sb[:].rearrange("p (q g d) -> p g q d", q=HEADS, g=G)[:, g]
                po = pay[:, r, g, 0:D].rearrange("p (q d) -> p q d", q=HEADS)
                yield Op(pool, [k, ("scatter", i - 2), ("q", i), ("q_psum", i)],
                         lambda e, xo=xo, oo=oo, po=po: e.tensor_tensor(po, xo, oo, ALU.add),
                         pool_us(D), ("x1", i) if g == G - 1 else None)
            M["attended", i] = M["x1", i]

        def row_tails(i):
            r = i % 2
            yield Op(pool, [("scatter", i - 2)], lambda e: e.iota(
                pay[:, r, :, :].bitcast(I32)[:, :, D + 2], pattern=[[1, G]], base=i * P * G, channel_multiplier=G),
                0.08, ("ids", i))
            yield Op(pool, [("scatter", i - 2)], lambda e: e.memset(pay[:, r, :, D + 3], 0.0), 0.04, ("pad", i))

        def gate(i):
            r = i % 2
            st = stat1[:, r]
            shift = yield from ln_stats(lambda g: pay[:, r, g, 0:D], st, lambda g: xn1[:, g * D:(g + 1) * D],
                                        [("x1", i), ("logits", i - 1)],
                                        pay[:, r, :, D + 1], pay[:, r, :, D], ("ln1_shift", i))
            for g in range(G):
                k = yield Op(act, [shift, ("logits", i - 1)], lambda e, g=g: e.activation(
                    xn1[:, g * D:(g + 1) * D], pay[:, r, g, 0:D], ACT.Identity,
                    scale=pay[:, r, g, D + 1:D + 2], bias=pay[:, r, g, D:D + 1]), act_us(D) + 0.1, ("xn1", i))
            for n in range(G * KD):
                k2 = yield Op(pe, [k, ("ident", 0), ("slots", i - 1),
                                     ("pick", picks_after(i - 1) - 1)], lambda e, n=n: e.transpose(
                    r_ps[:, n * P:(n + 1) * P], xn1[:, n * P:(n + 1) * P], ident[:]), 0.21)
            k = yield Op(act, [k2], lambda e: e.copy(xn1[:], r_ps[:]), act_us(G * D))
            turned = r_ps[0:E, 0:G * P]
            for k_ in range(KD):
                xt = xn1[:].rearrange("p (g k t) -> p g k t", g=G, k=KD)[:, :, k_, :]
                k = yield Op(pe, [k, ("gate", 0)], lambda e, k_=k_, xt=xt: e.matmul(
                    turned, gate_sb[:, k_, :], xt, start=k_ == 0, stop=k_ == KD - 1), pe32_us(G * P))
            k = yield Op(act, [k, ("gate", 0)], lambda e: e.activation(
                xn1[0:E, 0:G * P], turned, ACT.Identity, bias=gate_b_sb[:]), act_us(G * P))
            for g in range(G):
                yield Op(pe, [k], lambda e, g=g: e.transpose(
                    LG[:, g * E:(g + 1) * E], xn1[0:E, g * P:(g + 1) * P], ident[0:E, 0:E]),
                    0.21, ("logits", i) if g == G - 1 else None)

        def choose(i):
            v = [route[:, n, :].rearrange("p (g e) -> p g e", g=G) for n in range(6)]
            lg = LG.rearrange("p (g e) -> p g e", g=G)
            bc = lambda n: top[:, n, :].unsqueeze(2).to_broadcast([P, G, E])
            oh = onehot[:, i * G:(i + 1) * G, :]
            k = yield Op(dve, [("logits", i)], lambda e: e.tensor_reduce(top[:, 0, :], lg, AX_X, ALU.max), 0.08)
            k = yield Op(dve, [k], lambda e: e.tensor_tensor(v[0], lg, bc(0), ALU.is_ge), 0.08)
            k = yield Op(dve, [k, ("tables", 0)], lambda e: e.tensor_tensor(v[1], v[0], first_wins[:], ALU.mult), 0.08)
            k = yield Op(dve, [k], lambda e: e.tensor_reduce(top[:, 1, :], v[1], AX_X, ALU.max), 0.08)
            k = yield Op(dve, [k], lambda e: e.tensor_tensor(oh, v[1], bc(1), ALU.is_equal), 0.08, ("hot", i))
            for n in range(i * G, (i + 1) * G):
                k = yield Op(dve, [k], lambda e, n=n: e.tensor_tensor(
                    seen[:, n + 1, :], seen[:, n, :], onehot[:, n, :], ALU.add), 0.08,
                    ("seen", i) if n == (i + 1) * G - 1 else None)

        def rank(i):
            for g in range(G):
                n = i * G + g
                o = RK[:, g * E:(g + 1) * E]
                yield Op(pe, [("hot", i), ("before", 0)], lambda e, n=n, o=o: e.matmul(
                    o, before[:], onehot[:, n, :], start=True, stop=False), 0.06)
                yield Op(pe, [("seen", i)], lambda e, n=n, o=o: e.matmul(
                    o, ones_bf[:], seen[:, n, :], start=False, stop=True), 0.06)
            yield Op(pe, [], lambda e: e.matmul(CN, ones_bf[:], seen[:, (i + 1) * G, :], start=True, stop=True),
                     0.06, ("ranked", i))

        def scatter(i):
            r = i % 2
            v = [route[:, n, :].rearrange("p (g e) -> p g e", g=G) for n in range(6)]
            rk = RK.rearrange("p (g e) -> p g e", g=G)
            k = yield Op(dve, [("ranked", i)], lambda e: e.tensor_tensor(v[2], rk, region[:], ALU.add), 0.08)
            k = yield Op(dve, [k], lambda e: e.tensor_tensor(
                v[3], v[2], onehot[:, i * G:(i + 1) * G, :], ALU.mult), 0.08)
            k = yield Op(dve, [k], lambda e: e.tensor_reduce(slot_f[:], v[3], AX_X, ALU.add), 0.08)
            k = yield Op(dve, [k, ("scatter", i - 2)], lambda e: e.tensor_copy(slot_i[:, r, :], slot_f[:]),
                         0.08, ("slots", i))
            for g in range(G):
                yield Op(pool, [k, ("ids", i), ("pad", i), ("ln1_shift", i), ("x1", i)],
                         lambda e, g=g: e.indirect_dma_start(
                             out=sorted_rows, out_offset=bass.IndirectOffsetOnAxis(ap=slot_i[:, r, g:g + 1], axis=0),
                             in_=pay[:, r, g, :], in_offset=None, bounds_check=E * STRIDE - 1, oob_is_err=False),
                         1.04, ("scatter", i) if g == G - 1 else None, (s_scatter[r], 16 * G * (i // 2 + 1)), 130)

        def picks_after(i):
            n = (i + 1) * G * P - E * (P - 1)
            return NTILES if i == NG - 1 else max(0, (n - 1) // P + 1)

        def pack_of(j):
            first = picks_after(group_of[j] - 1)
            return first + (j - first) // SHARED * SHARED

        group_of = {}
        for i in range(NG):
            for j in range(picks_after(i - 1), picks_after(i)):
                group_of[j] = i

        def pick(j, i):
            k = yield Op(dve, [("ranked", i), ("tables", 0), ("pick", j - 1), ("plan", j - 1)],
                         lambda e: e.tensor_tensor_reduce(
                             left[:], CN[0:1, :], used[:], 1.0, -1e9, ALU.add, ALU.max, pick_v[:, 0:1]), 0.09)
            k = yield Op(dve, [k], lambda e: e.tensor_scalar(
                pick_hot[:], left[:], pick_v[:, 0:1], None, ALU.is_equal), 0.13)
            k = yield Op(dve, [k], lambda e: e.tensor_tensor_reduce(
                left[:], pick_hot[:], used[:], 1.0, 0.0, ALU.mult, ALU.add, pick_v[:, 1:2]), 0.09)
            yield Op(dve, [k], lambda e: e.tensor_scalar(
                plan[:, j:j + 1], pick_v[:, 1:2], -float(E), float(E - 1), ALU.mult, ALU.add), 0.07, ("plan", j))
            yield Op(dve, [k], lambda e: e.scalar_tensor_tensor(
                out=used[:], in0=pick_hot[:], scalar=-float(P), in1=used[:], op0=ALU.mult, op1=ALU.add),
                0.08, ("pick", j))

        def pack(first, n):
            e_, v = experts_of[:, 0:n], digits[:, 0:n]
            k = yield Op(dve, [("plan", first + n - 1)], lambda e: e.tensor_scalar(
                e_, plan[:, first:first + n], E - 1, None, ALU.bitwise_and), 0.08)
            k = yield Op(dve, [k, ("tables", 0)], lambda e: e.tensor_tensor(v, e_, shifts[:, 0:n], ALU.mult), 0.08)
            k = yield Op(dve, [k], lambda e: e.tensor_reduce(packed_f[:], v, AX_X, ALU.add), 0.08)
            yield Op(dve, [k], lambda e: e.tensor_copy(packed[:, first:first + 1], packed_f[:]),
                     0.08, ("packed", first))

        def fill():
            filler = prod[:, 0:2 * ROW].rearrange("p (r c) -> p r c", r=2)
            k = yield Op(dve, [("ranked", NG - 1)], lambda e: e.tensor_copy(count_i[:], CN[0:1, :]), 0.08)
            k2 = yield Op(pool, [("pv_sum", NG - 1, b) for b in DVE_BANDS],
                          lambda e: e.memset(filler, 0.0), 0.6)
            k2 = yield Op(pool, [k2], lambda e: e.memset(filler.bitcast(I32)[:, :, D + 2], SKIPPED_ROW), 0.1)
            for n in range(E):
                def issue(eng, n=n):
                    count = eng.value_load(count_i[0:1, n:n + 1], min_val=0, max_val=T)
                    row = nc.snap(count + n * STRIDE, min_val=0, max_val=E * STRIDE - 2 * P)
                    return eng.dma_start(
                        sorted_rows[bass.ds(row, 2 * P), :].rearrange("(p r) c -> p r c", r=2), filler)
                yield Op(sp, [k, k2], issue, 0.6, ("filled", 0), (s_fill, 16 * E), 260)

        def residuals():
            for i in range(NG):
                yield from residual(i)
                yield from row_tails(i)

        def gates():
            for i in range(NG):
                yield from gate(i)

        def routing():
            for i in range(NG):
                yield from choose(i)
                yield from rank(i)
                yield from scatter(i)

        def picks():
            for i in range(NG):
                first = picks_after(i - 1)
                for j in range(first, picks_after(i)):
                    yield from pick(j, i)
                    n = (j - first) % SHARED + 1
                    if n == SHARED or j + 1 == picks_after(i):
                        yield from pack(j + 1 - n, n)

        def fetch():
            for j in range(NTILES):
                r, i = j % FR, group_of[j]
                waits = [("plan", j), ("scatter", i), ("scatter", i - 1), ("stored", j - FR)]
                if i == NG - 1:
                    waits.append(("filled", 0))

                def issue_rows(eng, j=j, r=r):
                    u = eng.value_load(plan[0:1, j:j + 1], min_val=0, max_val=E * (T + P))
                    row = nc.snap((u & (E - 1)) * STRIDE + (u >> (E.bit_length() - 1)),
                                  min_val=0, max_val=E * STRIDE - P)
                    return eng.dma_start(rows[:, r, :], sorted_rows[bass.ds(row, P), :])

                def issue_bias(eng, j=j, r=r):
                    u = eng.value_load(plan[0:1, j:j + 1], min_val=0, max_val=E * (T + P))
                    e_ = nc.snap(u & (E - 1), min_val=0, max_val=E - 1)
                    return eng.dma_start(brow[:, j % 2, :].unsqueeze(1), bias_rows[bass.ds(e_, 1), :, :]
                                         .rearrange("e r w -> r e w"))
                yield Op(sp, waits, issue_rows, 0.7, ("rows", j), (s_rows[r], 16 * (j // FR + 1)), 130)
                yield Op(sp, [("plan", j), ("bias_rows", 0), ("up", j - 2), ("down_bias", j - 2)], issue_bias, 0.6,
                         ("brow", j), (s_brow[j % 2], 16 * (j // 2 + 1)), 8)

        def expert_inputs():
            for j in range(NTILES):
                r = j % FR
                k = yield Op(act, [("rows", j), ("expert_t", j - 1)], lambda e, r=r: e.activation(
                    xn2[:], rows[:, r, 0:D], ACT.Identity, scale=rows[:, r, D + 1:D + 2], bias=rows[:, r, D:D + 1]),
                    act_us(D) + 0.1)
                for k_ in range(KD):
                    k2 = yield Op(pe, [k, ("xt_lo", j - 1), ("ident", 0)], lambda e, k_=k_: e.transpose(
                        xt2_ps[:, k_ * P:(k_ + 1) * P], xn2[:, k_ * P:(k_ + 1) * P], ident[:]),
                        0.21, ("expert_t", j) if k_ == KD - 1 else None)
                hi, lo = xt_hi[:, j % 2], xt_lo[:, j % 2]
                k = yield Op(act, [k2, ("up", j - 2)], lambda e, hi=hi: e.copy(hi, xt2_ps), act_us(D), ("xt_hi", j))
                yield Op(dve, [k, ("up", j - 2)], lambda e, hi=hi, lo=lo: e.tensor_tensor(
                    lo, xt2_ps, hi, ALU.subtract), dve_us(D), ("xt_lo", j))

        weights_at = {}

        shared = {}

        def find_weights(eng, j):
            first, digit = pack_of(j), E.bit_length() - 1
            if j == first:
                shared[first] = nc.snap(eng.value_load(
                    packed[0:1, j:j + 1], min_val=0, max_val=E ** SHARED - 1), min_val=0, max_val=E ** SHARED - 1)
            weights_at[j] = nc.snap(((shared[first] >> (digit * (j - first))) & (E - 1)) * (KD * H),
                                    min_val=0, max_val=(E - 1) * KD * H)

        def up(j):
            def first(eng):
                find_weights(eng, j)
                return eng.matmul(h_ps[0][:, 0:P], brow[:, j % 2, 0:P], block_sum[:, 0, :], start=True, stop=False)
            for n in range(KH):
                c, at = n * P // HALF, n * P % HALF
                o = h_ps[c][:, at:at + P]
                if n == 0:
                    yield Op(pe, [("xt_lo", j), ("xt_hi", j), ("brow", j), ("weights", 0), ("weights", 1),
                                  ("packed", pack_of(j)), ("block_sum", 0), ("h_lo", j - 1, 0)], first,
                             0.5 if pack_of(j) == j else 0.06)
                else:
                    yield Op(pe, [("h_lo", j - 1, c)], lambda e, o=o, c=c, at=at: e.matmul(
                        o, brow[:, j % 2, at:at + P], block_sum[:, c, :], start=True, stop=False), pe_us(P))
                for k_ in range(KD):
                    for w, xt in ((w1_hi, xt_hi), (w1_hi, xt_lo), (w1_lo, xt_hi)):
                        last = k_ == KD - 1 and w is w1_lo
                        name = ("up_part", j, c) if last and (n + 1) * P % HALF == 0 else None
                        k = yield Op(pe, [], lambda e, o=o, n=n, k_=k_, w=w, xt=xt, last=last: e.matmul(
                            o, w[:, k_ * H + n * P:][:, bass.ds(weights_at[j], P)],
                            xt[:, j % 2, k_ * P:(k_ + 1) * P], start=False, stop=last), pe_us(P), name, address=0.07)
            M["up", j] = k

        def down(j):
            yield Op(pe, [("y", j - 1), ("h_lo", j, 0)], lambda e: e.matmul(
                y_ps, block_sum[:, BLOCKS - 1, :], brow[:, j % 2, 0:D], start=True, stop=False),
                     pe_us(D), ("down_bias", j))
            for n in range(KH):
                for h, w in ((h_hi, w2_hi), (h_hi, w2_lo), (h_lo, w2_hi)):
                    last = n == KH - 1 and h is h_lo
                    yield Op(pe, [("h_lo", j, n * P // HALF)], lambda e, n=n, h=h, w=w, last=last: e.matmul(
                        y_ps, h[j % 2][:, n * P:(n + 1) * P], w[:, n * D:][:, bass.ds(weights_at[j], D)],
                        start=False, stop=last), pe_us(D), ("down", j) if last else None,
                             address=0.07)

        STEADY = picks_after(NG - 6)

        def ups():
            for j in range(STEADY + 1):
                yield from up(j)

        def downs():
            for j in range(STEADY):
                yield from down(j)

        def ups_and_downs():
            for j in range(STEADY, NTILES):
                turns = [(down(j), 3)]
                if j + 1 < NTILES:
                    turns.insert(0, (up(j + 1), 1 + 3 * KD))
                marks = [None] * len(turns)
                while any(turns):
                    for t, turn in enumerate(turns):
                        for _ in range(turn[1] if turn else 0):
                            try:
                                marks[t] = yield turn[0].send(marks[t])
                            except StopIteration:
                                turns[t] = None
                                break

        def relus():
            for j in range(NTILES):
                for c in range(H // HALF):
                    cols = slice(c * HALF, (c + 1) * HALF)
                    k = yield Op(act, [("up_part", j, c), ("down", j - 2), ("weights", 0), ("weights", 1)],
                                 lambda e, j=j, c=c, cols=cols: e.activation(
                                     h_hi[j % 2][:, cols], h_ps[c][:], ACT.Relu), act_us(HALF))
                    yield Op(dve, [k, ("down", j - 2)], lambda e, j=j, c=c, cols=cols: e.scalar_tensor_tensor(
                        out=h_lo[j % 2][:, cols], in0=h_ps[c][:], scalar=0.0, in1=h_hi[j % 2][:, cols],
                        op0=ALU.max, op1=ALU.subtract), dve_us(HALF), ("h_lo", j, c))

        def results():
            for j in range(NTILES):
                r = j % FR
                k = yield Op(dve, [("down", j)], lambda e, r=r: e.scalar_tensor_tensor(
                    out=rows[:, r, 0:D], in0=y_ps, scalar=1.0 / (W_SCALE * W_SCALE), in1=rows[:, r, 0:D],
                    op0=ALU.mult, op1=ALU.add), dve_us(D), ("y", j))
                yield Op(pool, [k], lambda e, r=r: e.indirect_dma_start(
                    out=out, out_offset=bass.IndirectOffsetOnAxis(
                        ap=rows[:, r, :].bitcast(I32)[:, D + 2:D + 3], axis=0),
                    in_=rows[:, r, 0:D], in_offset=None, bounds_check=T - 1, oob_is_err=False),
                    1.04, ("stored", j), (s_out[r], 16 * (j // FR + 1)), 128)

        order = Order()
        M = order.marks
        order.merge([
            (1.0, load_x()), (1.0, load_context()), (0.6, small_constants()), (-1.0, small_inputs()),
            (-0.15, fill()), (-0.3, residuals()), (0.0, gates()), (0.02, routing()), (0.11, picks()),
            (-0.93, fetch()), (0.0, results()), (0.15, expert_inputs()), (-0.05, relus()),
            (0.0, downs()), (0.21, ups()), (0.15, ups_and_downs()), (-0.13, softmax()), (0.15, x_stats()),
            (0.3, queries(q_ps[:], "q_psum", lambda i: [("qk", i - 1)])),
            (-2.0, queries(q_sb[:], "q", lambda i: [("qk_pool", i - 1)])),
            (0.3, turned_values()), (0.15, top_products()), (0.15, top_sums()), (0.15, attention()),
            (-0.15, weights()),
        ])

        block = stack.enter_context(nc.Block())

        @block.sync
        def _(eng):
            sp.run(eng)
            for r in range(FR):
                eng.wait_ge(s_out[r], 16 * ((NTILES - r + FR - 1) // FR))

        @block.scalar
        def _(eng):
            act.run(eng)

        @block.vector
        def _(eng):
            dve.run(eng)

        @block.gpsimd
        def _(eng):
            pool.run(eng)

        @block.tensor
        def _(eng):
            pe.run(eng)


def kernel(x, ctx_1024, L0_ffn_gate_w, L0_ffn_gate_b, L0_ffn_w1, L0_ffn_b1, L0_ffn_w2, L0_ffn_b2):
    import concourse.bacc as bacc
    from concourse.bass_utils import run_bass_kernel_spmd

    B, S, D = x.shape
    E, H, _ = L0_ffn_w1.shape
    lay = np.ascontiguousarray
    arrays = {
        "x": lay(x).reshape(B * S, D),
        "ctx": lay(ctx_1024).reshape(B * S, D),
        "gate_w": lay(np.transpose(np.reshape(L0_ffn_gate_w, (E, D // P, P)), (2, 1, 0))),
        "gate_b": lay(np.reshape(L0_ffn_gate_b, (E, 1))),
        "w1": lay(np.transpose(np.reshape(L0_ffn_w1, (E, H, D // P, P)), (3, 0, 2, 1))).reshape(P, E, (D // P) * H),
        "b1": lay(L0_ffn_b1),
        "w2": lay(np.transpose(np.reshape(L0_ffn_w2, (E, D, H // P, P)), (3, 0, 2, 1))).reshape(P, E, (H // P) * D),
        "b2": lay(L0_ffn_b2),
    }
    nc = bacc.Bacc("TRN2", target_bir_lowering=False, num_devices=1)
    args = [nc.dram_tensor(n, a.shape, mybir.dt.from_np(a.dtype), kind="ExternalInput").ap() for n, a in arrays.items()]
    res = nc.dram_tensor("result", (B * S, D), F32, kind="ExternalOutput").ap()
    xattn_moe_kernel(nc, *args, res)
    got = run_bass_kernel_spmd(nc, [arrays], core_ids=[0])
    return got.results[0]["result"].reshape(B, S, D)
```
